# Optimizing a Trainium2 kernel written in Bass

```python
import numpy as np
import jax
import jax.numpy as jnp

def _softmax(x, axis=-1):
    return jax.nn.softmax(x, axis=axis)
def _gelu(x):
    return jax.nn.gelu(x, approximate=True)
def _silu(x):
    return jax.nn.silu(x)
def _sigmoid(x):
    return jax.nn.sigmoid(x)
def _layernorm(x, axis=-1, eps=1e-5):
    m = jnp.mean(x, axis=axis, keepdims=True)
    v = jnp.var(x, axis=axis, keepdims=True)
    return (x - m) / jnp.sqrt(v + eps)
def _scatter_add(tgt, idx, src, axis=0):
    return tgt.at[idx].add(src)
def _segment_sum(src, seg, n):
    return jax.ops.segment_sum(src, seg, n)

kernel_name = 'mk_adj_ffn_d1_adj_512_fc9088'

def setup_inputs(seed: int = 0):
    np.random.seed(seed)
    _w = jnp.asarray
    def _rec_inputs():
        import jax
        import jax.numpy as jnp
        _gk = jax.random.key(seed)
        x = -0.000929 + 1 * jax.random.normal(jax.random.fold_in(_gk, 1), (128, 128, 512), jnp.float32)
        _a = jax.random.bernoulli(jax.random.fold_in(_gk, 2), 0.0625, (128, 128))
        adj = _a.astype(jnp.int32)
        return x, adj
    x, adj = _rec_inputs()
    def _L0_gnn_setup():
        import jax, jax.numpy as jnp
        import numpy as np
        B, K, DIN, DOUT = (32, 64, 512, 512)
        key = jax.random.key(seed)
        k1, k2, k3, k4 = jax.random.split(key, 4)
        x = jax.random.normal(k1, (B, K, DIN), dtype=jnp.float32)
        adj = jax.random.randint(k2, (K, K), 0, 2, dtype=jnp.int32)
        W = jax.random.normal(k3, (DOUT, 2 * DIN), dtype=jnp.float32) * 0.02
        b = jax.random.normal(k4, (DOUT,), dtype=jnp.float32) * 0.02
        return {'x': x, 'adj': adj, 'W': W, 'b': b}
    _L0_gnn_all = _L0_gnn_setup()
    _L0_gnn_in = {k: v for k, v in _L0_gnn_all.items() if k in ('W', 'b', )}
    del _L0_gnn_all

    def _L0_ffn_setup():
        import jax, jax.numpy as jnp
        import numpy as np
        from jax import lax
        N, M, DIM, HEADS, TOPK = (4, 2048, 512, 8, 16)

        def _split_heads(t, h):
            n, m, c = t.shape
            return t.reshape(n, m, h, c // h).transpose(0, 2, 1, 3).reshape(n * h, m, c // h)
        key = jax.random.key(seed)
        ks = jax.random.split(key, 7)
        f = lambda k, s, sc=1.0: jax.random.normal(k, s, dtype=jnp.float32) * sc
        return {'x': f(ks[0], (N, M, DIM)), 'pos_w': f(ks[1], (DIM, 1, 3), 0.1), 'pos_b': f(ks[2], (DIM,), 0.02), 'qkv_w': f(ks[3], (3 * DIM, DIM), 0.02), 'qkv_b': f(ks[4], (3 * DIM,), 0.02), 'wo_w': f(ks[5], (DIM, DIM), 0.02), 'wo_b': f(ks[6], (DIM,), 0.02)}
    _L0_ffn_all = _L0_ffn_setup()
    _L0_ffn_in = {k: v for k, v in _L0_ffn_all.items() if k in ('pos_w', 'pos_b', 'qkv_w', 'qkv_b', 'wo_w', 'wo_b', )}
    del _L0_ffn_all

    return {
        "x": x,
        "adj": adj,
        "L0_gnn_W": _L0_gnn_in["W"],
        "L0_gnn_b": _L0_gnn_in["b"],
        "L0_ffn_pos_w": _L0_ffn_in["pos_w"],
        "L0_ffn_pos_b": _L0_ffn_in["pos_b"],
        "L0_ffn_qkv_w": _L0_ffn_in["qkv_w"],
        "L0_ffn_qkv_b": _L0_ffn_in["qkv_b"],
        "L0_ffn_wo_w": _L0_ffn_in["wo_w"],
        "L0_ffn_wo_b": _L0_ffn_in["wo_b"],
    }

def reference(x, adj, L0_gnn_W, L0_gnn_b, L0_ffn_pos_w, L0_ffn_pos_b, L0_ffn_qkv_w, L0_ffn_qkv_b, L0_ffn_wo_w, L0_ffn_wo_b):
    import jax
    import jax.numpy as jnp
    def _L0_gnn_ref(x, adj, W, b):
        import jax, jax.numpy as jnp
        import numpy as np
        B, K, DIN, DOUT = (32, 64, 512, 512)
        Din = x.shape[-1]
        Wi, Wj = (W[:, :Din], W[:, Din:])
        mi = jnp.einsum('bkd,od->bko', x, Wi)
        mj = jnp.einsum('bkd,od->bko', x, Wj)
        a = adj.astype(x.dtype)
        deg = a.sum(axis=1)
        out = deg[None, :, None] * (mi + b) + jnp.einsum('ij,bjo->bio', a, mj)
        return out

    def _L0_ffn_ref(x, pos_w, pos_b, qkv_w, qkv_b, wo_w, wo_b):
        import jax, jax.numpy as jnp
        import numpy as np
        from jax import lax
        N, M, DIM, HEADS, TOPK = (4, 2048, 512, 8, 16)

        def _split_heads(t, h):
            n, m, c = t.shape
            return t.reshape(n, m, h, c // h).transpose(0, 2, 1, 3).reshape(n * h, m, c // h)
        n, m, c = x.shape
        h = HEADS
        scale = c ** (-0.5)
        pos = lax.conv_general_dilated(x.transpose(0, 2, 1), pos_w, window_strides=(1,), padding=[(1, 1)], feature_group_count=c, dimension_numbers=('NCH', 'OIH', 'NCH'))
        x = x + (pos + pos_b[None, :, None]).transpose(0, 2, 1)
        qkv = x @ qkv_w.T + qkv_b
        q, k, v = jnp.split(qkv, [c, 2 * c], axis=-1)
        q = _split_heads(q, h)
        k = _split_heads(k, h)
        v = _split_heads(v, h)
        qd = lax.stop_gradient(q)
        kd = lax.stop_gradient(k)
        logits = jnp.einsum('bmd,bpd->bmp', qd * scale, kd)
        _, idx = lax.top_k(logits, TOPK)
        gather = jax.vmap(lambda t, i: t[i])
        k_sel = gather(k, idx)
        v_sel = gather(v, idx)
        attn = jax.nn.softmax(jnp.einsum('bmd,bmkd->bmk', q * scale, k_sel), axis=-1)
        out = jnp.einsum('bmk,bmkd->bmd', attn, v_sel)
        d = c // h
        out = out.reshape(n, h, m, d).transpose(0, 2, 1, 3).reshape(n, m, c)
        return out @ wo_w.T + wo_b

    x = x + _L0_gnn_ref(_layernorm(x, axis=-1), adj, L0_gnn_W, L0_gnn_b)
    x = x + _L0_ffn_ref(_layernorm(x, axis=-1), L0_ffn_pos_w, L0_ffn_pos_b, L0_ffn_qkv_w, L0_ffn_qkv_b, L0_ffn_wo_w, L0_ffn_wo_b)
    return x


_drawn_inputs = setup_inputs


def setup_inputs(seed=0):
    import zlib

    import numpy as np

    out = dict(_drawn_inputs(seed))
    spreads = {}
    factors = {'L0_ffn_pos_w': 8.0,
     'L0_ffn_pos_b': 8.0,
     'L0_ffn_qkv_w': 4.047,
     'L0_ffn_qkv_b': 8.0,
     'L0_ffn_wo_w': 4.002,
     'L0_ffn_wo_b': 8.0}
    for name, (base, spread) in spreads.items():
        noise = np.random.default_rng([zlib.crc32(name.encode()), seed]).standard_normal(out[name].shape)
        drawn = base * np.exp(spread * noise) if base else spread * noise
        out[name] = jnp.asarray(drawn.astype(out[name].dtype))
    for name, factor in factors.items():
        out[name] = (out[name] * factor).astype(out[name].dtype)
    return out
```

```python
from contextlib import ExitStack

import concourse.bass as bass
from concourse import mybir

F32, F16, I32 = mybir.dt.float32, mybir.dt.float16, mybir.dt.int32
ALU = mybir.AluOpType
ACT = mybir.ActivationFunctionType
AX = mybir.AxisListType

P = 128
D = 512
CT = D // P
ITEMS = 2
PAIRS = P // ITEMS
HEADS = 8
DH = D // HEADS
PH = HEADS // 2
TOPK = 16
EPS = 1e-5
WS = 64.0
LOGIT = float(D) ** -0.5 / (WS * WS)
TAKEN = -3.0e38
RING = 5
UNROLL = 4
FIRST, LAST = 2, PAIRS - 3
LOOPS = (LAST - FIRST + 1) // UNROLL


class Turn:

    def __init__(self, i, t):
        self.i, self.t, self.rolled = i, t, not isinstance(i, int)

    def has(self, d):
        return self.rolled or 0 <= self.t + d < PAIRS

    def count(self, per, events):
        const = per * self.t + events
        if not self.rolled:
            return const
        assert const > 0
        return self.i * (per * UNROLL) + const

    def dma(self, d):
        const = 16 * ((self.t + d) // UNROLL + 1)
        if not self.rolled:
            return const
        return self.i * 16 + const

    def slot(self, d, n):
        return (self.t + d) % n


def wait(eng, sem, value):
    if not isinstance(value, int) or value > 0:
        eng.wait_ge(sem, value)


CHUNKS = ([("z", j) for j in range(4)] + [("qk", 0), ("o", 0), ("v", 0), ("v", 1)]
          + [("qk", 1), ("o", 1), ("w", 0)]
          + [("qk", 2), ("o", 2), ("w", 1)]
          + [("qk", 3), ("o", 3), ("out", 0), ("y", 0), ("y", 1), ("out", 1)])
assert len(CHUNKS) % RING == 0


def chunk_exists(T, kind, j):
    return T.has({"z": 1, "w": 1, "y": 1, "qk": 0, "v": 0, "out": -1, "o": 0 if j >= 2 else -1}[kind])


def turns(engine, emit):
    for t in range(-2, FIRST):
        emit(Turn(0, t))
    with engine.Fori(0, LOOPS) as i:
        for t in range(FIRST, FIRST + UNROLL):
            emit(Turn(i, t))
    for t in range(FIRST + UNROLL * LOOPS, PAIRS + 1):
        emit(Turn(0, t))


def build(nc, x, adj, adj_t, gnn_wt, gnn_b, pos_w, pos_b, qkv_wt, qk_b, v_b, wo_wt, wo_b, out):
    ctx = ExitStack()
    with ctx:
        def sb(name, shape, dt=F32):
            return ctx.enter_context(nc.sbuf_tensor(name, shape, dt))

        def sem(name):
            return ctx.enter_context(nc.semaphore(name))

        stage = [sb(f"stage{i}", [P, 4 * D]) for i in range(2)]
        gw = [sb(f"gw_{n}", [P, 2 * CT, D], F16) for n in ("hi", "lo")]
        qkvw = [sb(f"qkvw_{n}", [P, CT, 3 * D], F16) for n in ("hi", "lo")]
        wow = [sb(f"wow_{n}", [P, CT, D], F16) for n in ("hi", "lo")]
        adj_i = sb("adj_i", [P, P], I32)
        adjt_i = sb("adjt_i", [P, P], I32)
        adj_f = sb("adj_f", [P, P])
        deg = sb("deg", [P, 1])
        mix = sb("mix", [P, 2 * P], F16)
        ident = sb("ident", [P, P])
        eps_c = sb("eps_c", [P, ITEMS])
        half_c = sb("half_c", [P, ITEMS])
        zero_c = sb("zero_c", [P, ITEMS])
        posw = sb("posw", [P, CT, 3])
        w1p = sb("w1p", [P, CT])
        posb = sb("posb", [P, CT])
        qkb = sb("qkb", [P, 2 * CT])
        vb = sb("vb", [P, CT])
        vb_wide = sb("vb_wide", [P, CT, P])
        degb = sb("degb", [P, D])
        outb = sb("outb", [P, D])
        X = [sb(f"X{i}", [P, ITEMS, D]) for i in range(UNROLL)]
        st1 = sb("st1", [P, ITEMS, 6])
        mv1 = sb("mv1", [P, ITEMS, 2])
        ve1, rstd1, nm1, shift1 = (sb(n, [P, ITEMS]) for n in ("ve1", "rstd1", "nm1", "shift1"))
        st2 = sb("st2", [P, ITEMS, 6])
        mv2 = sb("mv2", [P, ITEMS, 2])
        ve2, rstd2, nm2, shift2 = (sb(n, [P, ITEMS]) for n in ("ve2", "rstd2", "nm2", "shift2"))
        xn = sb("xn", [P, ITEMS, D])
        xh, xl = sb("xh", [P, ITEMS, D], F16), sb("xl", [P, ITEMS, D], F16)
        zh, zl = (sb(n, [P, 4, 4 * P], F16) for n in ("zh", "zl"))
        y = sb("y", [P, ITEMS, D])
        t = sb("t", [P, CT, ITEMS, P])
        ph = [sb(f"ph{i}", [P, CT, ITEMS, P], F16) for i in range(2)]
        pl = [sb(f"pl{i}", [P, CT, ITEMS, P], F16) for i in range(2)]
        vh = [sb(f"vh{i}", [P, ITEMS, D], F16) for i in range(2)]
        vl = [sb(f"vl{i}", [P, ITEMS, D], F16) for i in range(2)]
        qh, ql = (sb(n, [P, 2, ITEMS, P], F16) for n in ("qh", "ql"))
        M = sb("M", [P, 4, P])
        m16 = sb("m16", [P, 4, TOPK])
        d16 = sb("d16", [P, 4, TOPK])
        e16 = sb("e16", [P, 4, TOPK])
        s4, ln4, b4 = (sb(n, [P, 4]) for n in ("s4", "ln4", "b4"))
        E = sb("E", [P, 4, P])
        Pm = sb("Pm", [P, 4, P])
        th, tl = (sb(n, [P, 4, P], F16) for n in ("th", "tl"))
        oh = [sb(f"oh{i}", [P, PH, ITEMS, P], F16) for i in range(2)]
        ol = [sb(f"ol{i}", [P, PH, ITEMS, P], F16) for i in range(2)]
        ring = [ctx.enter_context(nc.psum_tensor(f"ring{i}", [P, D], F32)) for i in range(RING)]
        L = [ctx.enter_context(nc.psum_tensor(f"L{i}", [P, ITEMS, P], F32)) for i in range(2)]
        PT = ctx.enter_context(nc.psum_tensor("PT", [P, 4, P], F32))

        w_load = [sem(f"w_load{i}") for i in range(2)]
        c_load = sem("c_load")
        w_hi = sem("w_hi")
        w_lo = sem("w_lo")
        p_set = sem("p_set")
        v_set = sem("v_set")
        bias_mm = sem("bias_mm")
        ready = sem("ready")
        loaded = [sem(f"loaded{i}") for i in range(UNROLL)]
        stored = [sem(f"stored{i}") for i in range(UNROLL)]
        stat1 = sem("stat1")
        scale1 = sem("scale1")
        xn_done = sem("xn_done")
        xl_done = sem("xl_done")
        xdb_done = sem("xdb_done")
        z_mm, z_hi, z_lo = sem("z_mm"), sem("z_hi"), sem("z_lo")
        w_mm, x1_done = sem("w_mm"), sem("x1_done")
        stat2 = sem("stat2")
        scale2 = sem("scale2")
        y_done = sem("y_done")
        xb_done = sem("xb_done")
        y_mm, tap1 = sem("y_mm"), sem("tap1")
        conv = sem("conv")
        p_hi, p_lo = sem("p_hi"), sem("p_lo")
        v_mm, v_hi, v_lo = sem("v_mm"), sem("v_hi"), sem("v_lo")
        qk_mm, qk_hi, qk_lo = sem("qk_mm"), sem("qk_hi"), sem("qk_lo")
        l_mm = sem("l_mm")
        top = sem("top")
        d_done, e16_done, s_done, ln_done, b_done = (sem(n) for n in
                                                     ("d_done", "e16_done", "s_done", "ln_done", "b_done"))
        e_done, p_done = sem("e_done"), sem("p_done")
        t_mm, t_hi, t_lo = sem("t_mm"), sem("t_hi"), sem("t_lo")
        o_mm, o_hi, o_lo = sem("o_mm"), sem("o_hi"), sem("o_lo")
        out_mm, out_done = sem("out_mm"), sem("out_done")

        passed = sem("passed")
        pe_passed = sem("pe_passed")

        def freed(T, kind, j):
            return {"z": lambda: (z_lo, T.count(4, 4 + j + 1)),
                    "qk": lambda: (qk_lo, T.count(4, j + 1)),
                    "o": lambda: (o_lo, T.count(4, j - 2 + 1)),
                    "v": lambda: (v_lo, T.count(2, j + 1)),
                    "w": lambda: (x1_done, T.count(2, 2 + j + 1)),
                    "out": lambda: (out_done, T.count(2, -2 + j + 1)),
                    "y": lambda: (conv, T.count(8, 8 + 4 * (j + 1)))}[kind]()

        def bank(kind, j):
            return ring[CHUNKS.index((kind, j)) % RING]

        def wait_bank(T, pe, kind, j):
            n = CHUNKS.index((kind, j)) - RING
            while True:
                B = Turn(T.i, T.t + n // len(CHUNKS))
                if B.t < -1 and not B.rolled:
                    return
                before = CHUNKS[n % len(CHUNKS)]
                if chunk_exists(B, *before):
                    wait(pe, *freed(B, *before))
                    return
                n -= RING

        blocks = [(gnn_wt[:, 0:CT, :], [w[:, 0:CT, :] for w in gw]),
                  (gnn_wt[:, CT:2 * CT, :], [w[:, CT:2 * CT, :] for w in gw])]
        blocks += [(qkv_wt[:, :, D * j:D * (j + 1)], [w[:, :, D * j:D * (j + 1)] for w in qkvw]) for j in range(3)]
        blocks += [(wo_wt[:, :, :], [w[:, :, :] for w in wow])]
        NB = len(blocks)

        def staged(n):
            return stage[n % 2][:, :].rearrange("p (a b) -> p a b", b=D)

        smalls = [(adj_i[:, :], adj), (adjt_i[:, :], adj_t), (posw[:, :, :], pos_w), (posb[:, :], pos_b),
                  (qkb[:, :], qk_b), (vb[:, :], v_b), (degb[:, :], gnn_b.to_broadcast((P, D))),
                  (outb[:, :], wo_b.to_broadcast((P, D)))]

        block = ctx.enter_context(nc.Block())

        @block.sync
        def _(sp):
            def load(T, d):
                if not T.has(d):
                    return
                if T.rolled or T.has(d - UNROLL):
                    wait(sp, stored[T.slot(d, UNROLL)], T.dma(d - UNROLL))
                sp.dma_start(X[T.slot(d, UNROLL)][:, :, :], entries(x, T, d)).then_inc(loaded[T.slot(d, UNROLL)], 16)

            def entries(array, T, d):
                a = array.rearrange("(u b) k d -> u k b d", b=ITEMS)
                return a[T.i * UNROLL + (T.t + d)]

            for dst, src in smalls:
                sp.dma_start(dst, src).then_inc(c_load, 16)
            for n, (src, _) in enumerate(blocks):
                if n >= 2:
                    sp.wait_ge(w_lo, n - 1)
                if n == NB - 1:
                    sp.wait_ge(w_lo, n)
                sp.dma_start(staged(n), src).then_inc(w_load[n % 2], 16)

            def turn(T):
                load(T, 2)
                if T.has(-1):
                    wait(sp, out_done, T.count(2, 0))
                    sp.dma_start(entries(out, T, -1), X[T.slot(-1, UNROLL)][:, :, :])\
                        .then_inc(stored[T.slot(-1, UNROLL)], 16)

            turns(sp, turn)
            for j in range(UNROLL):
                sp.wait_ge(stored[j], 16 * (PAIRS // UNROLL))

        @block.tensor
        def _(pe):
            mm = nc.tensor.matmul

            pe.wait_ge(v_set, 2)
            pe.wait_ge(w_load[(NB - 1) % 2], 16 * ((NB + 1) // 2))
            wo_f = staged(NB - 1)
            for c in range(CT):
                last = mm(ring[0][:, :], vb_wide[:, c, :], wo_f[:, c, :], start=c == 0, stop=c == CT - 1)
            last.then_inc(bias_mm, 1)
            pe.wait_ge(ready, 1)

            def three(dst, a, b, first, last):
                mm(dst, a[0], b[0], start=first, stop=False)
                mm(dst, a[0], b[1], start=False, stop=False)
                return mm(dst, a[1], b[0], start=False, stop=last)

            def mix_tokens(T, j):
                item, half = divmod(j, 2)
                if j == 0:
                    wait(pe, xl_done, T.count(1, 2))
                wait_bank(T, pe, "z", j)
                dst = bank("z", j)[:, :].rearrange("p (a b) -> p a b", a=2)
                for a in range(2):
                    c = 2 * half + a
                    mm(dst[:, a, :], xh[:, item, c * P:(c + 1) * P], mix[:, :], start=True, stop=False)
                    last = mm(dst[:, a, :], xl[:, item, c * P:(c + 1) * P], mix[:, :], start=False, stop=True)
                last.then_inc(z_mm, 1)

            def graph_weights(T, item):
                wait(pe, z_lo, T.count(4, 4 + 2 * item + 2))
                wait_bank(T, pe, "w", item)
                for n in range(2 * CT):
                    side, c = divmod(n, CT)
                    col = (c % 2) * 2 * P + side * P
                    lhs = [z[:, 2 * item + c // 2, col:col + P] for z in (zh, zl)]
                    last = three(bank("w", item)[:, :], lhs, [w[:, n, :] for w in gw], n == 0, n == 2 * CT - 1)
                last.then_inc(w_mm, 1)

            def turn_y(T, j):
                wait(pe, y_done, T.count(2, 4))
                wait_bank(T, pe, "y", j)
                dst = bank("y", j)[:, :].rearrange("p (a i k) -> p a i k", a=2, i=ITEMS)
                for a in range(2):
                    for item in range(ITEMS):
                        c = 2 * j + a
                        last = nc.tensor.transpose(dst[:, a, item, :], y[:, item, c * P:(c + 1) * P], ident[:, :])
                last.then_inc(y_mm, 1)

            def values(T, item):
                wait(pe, p_lo, T.count(2, 2))
                wait_bank(T, pe, "v", item)
                s = T.slot(0, 2)
                for c in range(CT):
                    last = three(bank("v", item)[:, :], [a[s][:, c, item, :] for a in (ph, pl)],
                                 [w[:, c, 2 * D:3 * D] for w in qkvw], c == 0, c == CT - 1)
                last.then_inc(v_mm, 1)

            def queries_keys(T, f):
                wait(pe, p_lo, T.count(2, 2))
                wait_bank(T, pe, "qk", f)
                s = T.slot(0, 2)
                for side in range(2):
                    col = side * D + f * P
                    for c in range(CT):
                        last = three(bank("qk", f)[:, side * 2 * P:(side + 1) * 2 * P],
                                     [w[:, c, col:col + P] for w in qkvw],
                                     [a[s][:, c, :, :] for a in (ph, pl)], c == 0, c == CT - 1)
                last.then_inc(qk_mm, 1)

            def logits(T, f):
                wait(pe, e_done, T.count(4, f))
                wait(pe, qk_lo, T.count(4, f + 1))
                if T.rolled:
                    pe.sem_inc(pe_passed, 1)
                for item in range(ITEMS):
                    for h in range(2):
                        r = slice(h * DH, (h + 1) * DH)
                        last = three(L[h][:, item, :], [a[r, 0, item, :] for a in (qh, ql)],
                                     [a[r, 1, item, :] for a in (qh, ql)], True, True)
                last.then_inc(l_mm, 1)

            def turn_probs(T, f):
                wait(pe, p_done, T.count(4, f))
                wait(pe, t_lo, T.count(4, f - 1))
                for j in range(4):
                    last = nc.tensor.transpose(PT[:, j, :], Pm[:, j, :], ident[:, :])
                last.then_inc(t_mm, 1)

            def weighted_values(T, f):
                s = T.slot(0 if f >= 2 else -1, 2)
                head = 2 * ((f - 2) % PH)
                wait(pe, v_lo, T.count(2, 2 if f >= 2 else 0))
                wait(pe, t_lo, T.count(4, f - 1))
                wait_bank(T, pe, "o", f)
                for item in range(ITEMS):
                    for h in range(2):
                        col = slice((head + h) * DH, (head + h + 1) * DH)
                        last = three(bank("o", f)[h * DH:(h + 1) * DH, item * P:(item + 1) * P],
                                     [v[s][:, item, col] for v in (vh, vl)],
                                     [a[:, 2 * item + h, :] for a in (th, tl)], True, True)
                last.then_inc(o_mm, 1)

            def project(T, item):
                s = T.slot(-1, 2)
                wait(pe, o_lo, T.count(4, 0))
                wait_bank(T, pe, "out", item)
                for c in range(CT):
                    last = three(bank("out", item)[:, :], [o[s][:, c, item, :] for o in (oh, ol)],
                                 [w[:, c, :] for w in wow], c == 0, c == CT - 1)
                last.then_inc(out_mm, 1)

            def turn(T):
                for f in range(PH):
                    if f == 0 and T.has(1):
                        for j in range(4):
                            mix_tokens(T, j)
                    if T.has(0):
                        queries_keys(T, f)
                    if T.has(0 if f >= 2 else -1):
                        weighted_values(T, f)
                    if f == 0 and T.has(0):
                        values(T, 0)
                    if f in (1, 2) and T.has(1):
                        graph_weights(T, f - 1)
                    if f == 3 and T.has(-1):
                        project(T, 0)
                    if T.has(0):
                        logits(T, f)
                    if T.has(0 if f >= 1 else -1):
                        turn_probs(T, f)
                    if f == 0 and T.has(0):
                        values(T, 1)
                    if f == 3 and T.has(1):
                        turn_y(T, 0)
                        turn_y(T, 1)
                    if f == 3 and T.has(-1):
                        project(T, 1)

            turns(pe, turn)

        @block.scalar
        def _(act):
            op = nc.scalar.activation
            nc.scalar.preload_act_table_set("natural_log_exp_and_others")
            for n, (_, dst) in enumerate(blocks):
                act.wait_ge(w_load[n % 2], 16 * (n // 2 + 1))
                op(dst[0], staged(n), ACT.Copy, scale=WS).then_inc(w_hi, 1)
            act.wait_ge(ready, 1)

            def normalize1(T):
                Xu = X[T.slot(2, UNROLL)]
                wait(act, scale1, T.count(4, 12))
                wait(act, xl_done, T.count(1, 2))
                for item in range(ITEMS):
                    op(xn[:, item, :], Xu[:, item, :], ACT.Identity, scale=rstd1[:, item:item + 1],
                       bias=shift1[:, item:item + 1]).then_inc(xn_done, 1)
                wait(act, z_mm, T.count(4, 8))
                wait(act, xn_done, T.count(3, 8))
                op(xh[:, :, :], xn[:, :, :], ACT.Copy).then_inc(xn_done, 1)

            def z_split(T, j):
                wait(act, z_mm, T.count(4, 4 + j + 1))
                if j == 0:
                    wait(act, w_mm, T.count(2, 2))
                op(zh[:, j, :], bank("z", j)[:, :], ACT.Copy).then_inc(z_hi, 1)

            def normalize2(T, item):
                wait(act, scale2, T.count(8, 8 + 4 * item + 4))
                if item == 0:
                    wait(act, y_mm, T.count(2, 2))
                op(y[:, item, :], X[T.slot(1, UNROLL)][:, item, :], ACT.Identity, scale=rstd2[:, item:item + 1],
                   bias=shift2[:, item:item + 1]).then_inc(y_done, 1)

            def middle_tap(T, j):
                wait(act, y_mm, T.count(2, 2 + j + 1))
                wait(act, p_lo, T.count(2, j + 1))
                src = bank("y", j)[:, :].rearrange("p (a i k) -> p a i k", a=2, i=ITEMS)
                for a in range(2):
                    c = 2 * j + a
                    last = op(t[:, c, :, :], src[:, a, :, :], ACT.Identity, scale=w1p[:, c:c + 1],
                              bias=posb[:, c:c + 1])
                last.then_inc(tap1, 1)

            def pos_split(T, j):
                wait(act, conv, T.count(8, 8 + 4 * (j + 1)))
                wait(act, qk_mm, T.count(4, 0))
                op(ph[T.slot(1, 2)][:, 2 * j:2 * j + 2, :, :], t[:, 2 * j:2 * j + 2, :, :], ACT.Copy).then_inc(p_hi, 1)

            def v_split(T, item):
                wait(act, v_mm, T.count(2, item + 1))
                wait(act, o_mm, T.count(4, -4))
                op(vh[T.slot(0, 2)][:, item, :], bank("v", item)[:, :], ACT.Copy).then_inc(v_hi, 1)

            def qk_split(T, f):
                wait(act, qk_mm, T.count(4, f + 1))
                wait(act, l_mm, T.count(4, f))
                for side in range(2):
                    n = side * CT + f
                    last = op(qh[:, side, :, :], bank("qk", f)[:, side * 2 * P:(side + 1) * 2 * P], ACT.Identity,
                              bias=qkb[:, n:n + 1])
                last.then_inc(qk_hi, 1)

            def soft_sum(T, f):
                wait(act, d_done, T.count(4, f))
                wait(act, s_done, T.count(4, f - 1))
                op(e16[:, :, :], d16[:, :, :], ACT.Exp, scale=LOGIT).then_inc(e16_done, 1)

            def soft_log(T, f):
                wait(act, s_done, T.count(4, f))
                wait(act, b_done, T.count(4, f - 1))
                op(ln4[:, :], s4[:, :], ACT.Ln).then_inc(ln_done, 1)

            def soft_exp(T, f):
                wait(act, b_done, T.count(4, f))
                wait(act, p_done, T.count(4, f - 1))
                for j in range(4):
                    item, h = divmod(j, 2)
                    last = op(E[:, j, :], L[h][:, item, :], ACT.Exp, scale=LOGIT, bias=b4[:, j:j + 1])
                last.then_inc(e_done, 1)

            def probs_split(T, f):
                wait(act, t_mm, T.count(4, f))
                wait(act, o_mm, T.count(4, f - 1))
                op(th[:, :, :], PT[:, :, :], ACT.Copy).then_inc(t_hi, 1)

            def o_split(T, f):
                s = T.slot(0 if f >= 2 else -1, 2)
                wait(act, o_mm, T.count(4, f - 1))
                if f == 2:
                    wait(act, out_mm, T.count(2, -2))
                op(oh[s][:, (f - 2) % PH, :, :], bank("o", f)[:, 0:ITEMS * P], ACT.Copy).then_inc(o_hi, 1)

            def turn(T):
                for f in range(PH):
                    softmax = T.has(0 if f >= 1 else -1)
                    if softmax:
                        soft_sum(T, f)
                    if f == 0 and T.has(1):
                        for j in range(4):
                            z_split(T, j)
                    if T.has(0):
                        qk_split(T, f)
                    if softmax:
                        soft_log(T, f)
                    if T.has(0 if f >= 2 else -1):
                        o_split(T, f)
                    if softmax:
                        soft_exp(T, f)
                    if f == 0 and T.has(0):
                        v_split(T, 0)
                    if softmax:
                        probs_split(T, f)
                    if f == 0 and T.has(0):
                        v_split(T, 1)
                    if f in (1, 2) and T.has(1):
                        normalize2(T, f - 1)
                    if f == 3 and T.has(1):
                        for j in range(2):
                            middle_tap(T, j)
                    if f == 3 and T.has(2):
                        normalize1(T)
                    if f == 3 and T.has(1):
                        for j in range(2):
                            pos_split(T, j)

            turns(act, turn)

        @block.vector
        def _(dve):
            stt, tt = nc.vector.scalar_tensor_tensor, nc.vector.tensor_tensor

            dve.wait_ge(c_load, 16 * len(smalls))
            dve.wait_ge(p_set, 3)
            nc.vector.memset(vb_wide[:, :, :], 1.0).then_inc(v_set, 1)
            dve.wait_ge(v_set, 1)
            tt(vb_wide[:, :, :], vb_wide[:, :, :], vb[:, :].rearrange("p (c o) -> p c o", o=1).to_broadcast((P, CT, P)),
               ALU.mult).then_inc(v_set, 1)
            nc.vector.tensor_copy(adj_f[:, :], adj_i[:, :]).then_inc(v_set, 1)
            nc.vector.tensor_copy(mix[:, P:2 * P], adjt_i[:, :])
            nc.vector.tensor_scalar(w1p[:, :], posw[:, :, 1], 1.0, None, ALU.add)
            nc.vector.tensor_scalar(qkb[:, :], qkb[:, :], WS, None, ALU.mult)
            dve.wait_ge(v_set, 3)
            nc.vector.tensor_reduce(deg[:, :], adj_f[:, :], AX.X, ALU.add).then_inc(v_set, 1)
            dve.wait_ge(v_set, 4)
            nc.vector.tensor_scalar(mix[:, 0:P], ident[:, :], deg[:, 0:1], None, ALU.mult)
            nc.vector.tensor_scalar(degb[:, :], degb[:, :], deg[:, 0:1], None, ALU.mult)
            for n, (_, dst) in enumerate(blocks):
                if n == NB - 1:
                    dve.wait_ge(bias_mm, 1)
                    tt(outb[:, :], ring[0][:, :], outb[:, :], ALU.add)
                dve.wait_ge(w_hi, n + 1)
                stt(out=dst[1], in0=staged(n), scalar=WS, in1=dst[0], op0=ALU.mult, op1=ALU.subtract).then_inc(w_lo, 1)
            dve.wait_ge(w_lo, NB)
            nc.vector.memset(st1[:, :, :], 0.0).then_inc(ready, 1)
            dve.wait_ge(ready, 1)

            def apart(sem, value):
                if not isinstance(value, int) or value > 0:
                    dve.wait_ge(sem, value)
                    dve.sem_inc(passed, 1)

            def stats1(T):
                Xu = X[T.slot(2, UNROLL)]
                wait(dve, scale1, T.count(4, 8))
                apart(loaded[T.slot(2, UNROLL)], T.dma(2))
                for item in range(ITEMS):
                    nc.vector.bn_stats(st1[:, item, :], Xu[:, item, :]).then_inc(stat1, 1)
                for item in range(ITEMS):
                    apart(stat1, T.count(4, 8 + item + 1))
                    nc.vector.bn_aggr(mv1[:, item, :], st1[:, item, :]).then_inc(stat1, 1)

            def z_split(T, j):
                wait(dve, z_hi, T.count(4, 4 + j + 1))
                tt(zl[:, j, :], bank("z", j)[:, :], zh[:, j, :], ALU.subtract).then_inc(z_lo, 1)

            def residual(T, item):
                Xu = X[T.slot(1, UNROLL)]
                wait(dve, xdb_done, T.count(1, 2))
                wait(dve, w_mm, T.count(2, 2 + item + 1))
                stt(out=Xu[:, item, :], in0=bank("w", item)[:, :], scalar=1 / WS, in1=Xu[:, item, :], op0=ALU.mult,
                    op1=ALU.add).then_inc(x1_done, 1)
                wait(dve, scale2, T.count(8, 4 * item + 4))
                apart(x1_done, T.count(2, 2 + item + 1))
                nc.vector.bn_stats(st2[:, item, :], Xu[:, item, :]).then_inc(stat2, 1)
                apart(stat2, T.count(4, 4 + 2 * item + 1))
                nc.vector.bn_aggr(mv2[:, item, :], st2[:, item, :]).then_inc(stat2, 1)

            def outer_taps(T, j):
                src = bank("y", j)[:, :].rearrange("p (a i k) -> p a i k", a=2, i=ITEMS)
                wait(dve, tap1, T.count(2, 2 + j + 1))
                for a in range(2):
                    c = 2 * j + a
                    stt(out=t[:, c, :, 1:P], in0=src[:, a, :, 0:P - 1], scalar=posw[:, c, 0:1], in1=t[:, c, :, 1:P],
                        op0=ALU.mult, op1=ALU.add).then_inc(conv, 1)
                for a in range(2):
                    c = 2 * j + a
                    wait(dve, conv, T.count(8, 8 + 4 * j + a + 1))
                    stt(out=t[:, c, :, 0:P - 1], in0=src[:, a, :, 1:P], scalar=posw[:, c, 2:3],
                        in1=t[:, c, :, 0:P - 1], op0=ALU.mult, op1=ALU.add).then_inc(conv, 1)

            def v_split(T, item):
                s = T.slot(0, 2)
                wait(dve, v_hi, T.count(2, item + 1))
                tt(vl[s][:, item, :], bank("v", item)[:, :], vh[s][:, item, :], ALU.subtract).then_inc(v_lo, 1)

            def qk_split(T, f):
                wait(dve, qk_hi, T.count(4, f + 1))
                for side in range(2):
                    n = side * CT + f
                    last = stt(out=ql[:, side, :, :], in0=bank("qk", f)[:, side * 2 * P:(side + 1) * 2 * P],
                               scalar=qkb[:, n:n + 1], in1=qh[:, side, :, :], op0=ALU.add, op1=ALU.subtract)
                last.then_inc(qk_lo, 1)

            def select(T, f):
                n = 16 * (f - 1)

                def of(j):
                    item, h = divmod(j, 2)
                    return L[h][:, item, :]

                wait(dve, ln_done, T.count(4, f - 1))
                apart(l_mm, T.count(4, f))
                for j in range(4):
                    nc.vector.max(m16[:, j, 0:8], of(j)).then_inc(top, 1)
                for j in range(4):
                    if j in (0, 3):
                        apart(top, T.count(64, n + (3 if j == 0 else 4)))
                    nc.vector.match_replace(M[:, j, :], m16[:, j, 0:8], of(j), TAKEN).then_inc(top, 1)
                for j in range(4):
                    if j in (0, 3):
                        apart(top, T.count(64, n + 4 + (3 if j == 0 else 4)))
                    nc.vector.max(m16[:, j, 8:16], M[:, j, :]).then_inc(top, 1)
                for j in range(4):
                    if j in (0, 3):
                        apart(top, T.count(64, n + 8 + (3 if j == 0 else 4)))
                    nc.vector.match_replace(M[:, j, :], m16[:, j, 8:16], M[:, j, :], TAKEN).then_inc(top, 1)
                wait(dve, e16_done, T.count(4, f - 1))
                tt(d16[:, :, :], m16[:, :, :], m16[:, :, 0:1].to_broadcast((P, 4, TOPK)), ALU.subtract)\
                    .then_inc(d_done, 1)

            def soft_sum(T, f):
                wait(dve, e16_done, T.count(4, f))
                nc.vector.tensor_reduce(s4[:, :], e16[:, :, :], AX.X, ALU.add).then_inc(s_done, 1)

            def soft_bias(T, f):
                wait(dve, ln_done, T.count(4, f))
                wait(dve, e_done, T.count(4, f - 1))
                stt(out=b4[:, :], in0=m16[:, :, 0], scalar=-LOGIT, in1=ln4[:, :], op0=ALU.mult, op1=ALU.subtract)\
                    .then_inc(b_done, 1)

            def keep(T, f):
                wait(dve, e_done, T.count(4, f))
                wait(dve, t_mm, T.count(4, f - 1))
                stt(out=Pm[:, :, :], in0=M[:, :, :], scalar=TAKEN, in1=E[:, :, :], op0=ALU.is_equal, op1=ALU.mult)\
                    .then_inc(p_done, 1)

            def probs_split(T, f):
                wait(dve, t_hi, T.count(4, f))
                tt(tl[:, :, :], PT[:, :, :], th[:, :, :], ALU.subtract).then_inc(t_lo, 1)

            def o_split(T, f):
                s = T.slot(0 if f >= 2 else -1, 2)
                wait(dve, o_hi, T.count(4, f - 1))
                tt(ol[s][:, (f - 2) % PH, :, :], bank("o", f)[:, 0:ITEMS * P].rearrange("p (i k) -> p i k", i=ITEMS),
                   oh[s][:, (f - 2) % PH, :, :], ALU.subtract).then_inc(o_lo, 1)

            def finish(T, item):
                Xu = X[T.slot(-1, UNROLL)]
                wait(dve, xb_done, T.count(2, -2 + item + 1))
                wait(dve, out_mm, T.count(2, -2 + item + 1))
                stt(out=Xu[:, item, :], in0=bank("out", item)[:, :], scalar=1 / (WS * WS), in1=Xu[:, item, :],
                    op0=ALU.mult, op1=ALU.add).then_inc(out_done, 1)

            def turn(T):
                for f in range(PH):
                    softmax = T.has(0 if f >= 1 else -1)
                    if softmax:
                        select(T, f)
                    if f == 0 and T.has(1):
                        for j in range(4):
                            z_split(T, j)
                    if T.has(0):
                        qk_split(T, f)
                    if softmax:
                        soft_sum(T, f)
                    if T.has(0 if f >= 2 else -1):
                        o_split(T, f)
                    if softmax:
                        soft_bias(T, f)
                    if f == 3 and T.has(2):
                        stats1(T)
                    if f == 0 and T.has(0):
                        v_split(T, 0)
                    if softmax:
                        keep(T, f)
                    if f in (1, 2) and T.has(1):
                        residual(T, f - 1)
                    if f == 3 and T.has(-1):
                        finish(T, 0)
                    if softmax:
                        probs_split(T, f)
                    if f == 0 and T.has(0):
                        v_split(T, 1)
                    if f == 3 and T.has(1):
                        outer_taps(T, 0)
                        outer_taps(T, 1)
                    if f == 3 and T.has(-1):
                        finish(T, 1)

            turns(dve, turn)

        @block.gpsimd
        def _(pool):
            tt = nc.gpsimd.tensor_tensor
            nc.gpsimd.memset(ident[:, :], 0.0).then_inc(p_set, 1)
            nc.gpsimd.memset(eps_c[:, :], EPS)
            nc.gpsimd.memset(zero_c[:, :], 0.0)
            nc.gpsimd.memset(half_c[:, :], -0.5).then_inc(p_set, 1)
            pool.wait_ge(p_set, 2)
            nc.gpsimd.affine_select(out=ident[:, :], in_=ident[:, :], compare_op=ALU.not_equal, fill=1.0, base=0,
                                    pattern=[[-1, P]], channel_multiplier=1).then_inc(p_set, 1)
            pool.wait_ge(ready, 1)

            def scales(T, mv, ve, rstd, nm, shift, sem, per, at):
                tt(ve, mv[1], eps_c[:, 0:ve.shape[1]], ALU.add).then_inc(sem, 1)
                wait(pool, sem, T.count(per, at + 1))
                tt(rstd, ve, half_c[:, 0:ve.shape[1]], ALU.pow).then_inc(sem, 1)
                wait(pool, sem, T.count(per, at + 2))
                tt(nm, mv[0], rstd, ALU.mult).then_inc(sem, 1)
                wait(pool, sem, T.count(per, at + 3))
                tt(shift, zero_c[:, 0:ve.shape[1]], nm, ALU.subtract).then_inc(sem, 1)

            def normalize1(T):
                wait(pool, stat1, T.count(4, 12))
                wait(pool, xn_done, T.count(3, 6))
                scales(T, (mv1[:, :, 0], mv1[:, :, 1]), ve1[:, :], rstd1[:, :], nm1[:, :], shift1[:, :], scale1, 4, 8)
                wait(pool, xn_done, T.count(3, 9))
                wait(pool, z_mm, T.count(4, 8))
                tt(xl[:, :, :], xn[:, :, :], xh[:, :, :], ALU.subtract).then_inc(xl_done, 1)
                Xu = X[T.slot(2, UNROLL)]
                for item in range(ITEMS):
                    last = tt(Xu[:, item, :], Xu[:, item, :], degb[:, :], ALU.add)
                last.then_inc(xdb_done, 1)

            def normalize2(T, item):
                r = slice(item, item + 1)
                wait(pool, stat2, T.count(4, 4 + 2 * item + 2))
                wait(pool, y_done, T.count(2, item + 1))
                scales(T, (mv2[:, r, 0], mv2[:, r, 1]), ve2[:, r], rstd2[:, r], nm2[:, r], shift2[:, r], scale2, 8,
                       8 + 4 * item)
                wait(pool, y_done, T.count(2, 2 + item + 1))
                Xu = X[T.slot(1, UNROLL)]
                tt(Xu[:, item, :], Xu[:, item, :], outb[:, :], ALU.add).then_inc(xb_done, 1)

            def pos_split(T, j):
                c = slice(2 * j, 2 * j + 2)
                s = T.slot(1, 2)
                wait(pool, p_hi, T.count(2, 2 + j + 1))
                tt(pl[s][:, c, :, :], t[:, c, :, :], ph[s][:, c, :, :], ALU.subtract).then_inc(p_lo, 1)

            def turn(T):
                if T.has(1):
                    for item in range(ITEMS):
                        normalize2(T, item)
                if T.has(2):
                    normalize1(T)
                if T.has(1):
                    for j in range(2):
                        pos_split(T, j)

            turns(pool, turn)


_OUT = ("out_0_dram", (P, P, D))


def kernel(x, adj, L0_gnn_W, L0_gnn_b, L0_ffn_pos_w, L0_ffn_pos_b, L0_ffn_qkv_w, L0_ffn_qkv_b, L0_ffn_wo_w,
           L0_ffn_wo_b):
    import numpy as np
    import concourse.bacc as bacc
    from concourse.bass_utils import run_bass_kernel_spmd

    def columns(w):
        w = np.asarray(w)
        return w.T.reshape(w.shape[1] // P, P, w.shape[0]).transpose(1, 0, 2)

    def by_channel(v):
        v = np.asarray(v)
        return v.reshape((v.shape[0] // P, P) + v.shape[1:]).swapaxes(0, 1)

    qkv_b = np.asarray(L0_ffn_qkv_b)
    inputs = {
        "x": x, "adj": adj, "adj_t": np.asarray(adj).T, "gnn_wt": columns(L0_gnn_W),
        "gnn_b": np.asarray(L0_gnn_b).reshape(1, D), "pos_w": by_channel(np.asarray(L0_ffn_pos_w).reshape(D, 3)),
        "pos_b": by_channel(L0_ffn_pos_b), "qkv_wt": columns(L0_ffn_qkv_w), "qk_b": by_channel(qkv_b[:2 * D]),
        "v_b": by_channel(qkv_b[2 * D:]), "wo_wt": columns(L0_ffn_wo_w), "wo_b": np.asarray(L0_ffn_wo_b).reshape(1, D),
    }
    nc = bacc.Bacc("TRN2", target_bir_lowering=False, num_devices=1)
    arrays, args = {}, []
    for name, a in inputs.items():
        a = np.ascontiguousarray(a)
        arrays[f"in_{name}_dram"] = a
        args.append(nc.dram_tensor(f"in_{name}_dram", a.shape, mybir.dt.from_np(a.dtype), kind="ExternalInput").ap())
    args.append(nc.dram_tensor(_OUT[0], _OUT[1], F32, kind="ExternalOutput").ap())
    build(nc, *args)
    return run_bass_kernel_spmd(nc, [arrays], core_ids=[0]).results[0][_OUT[0]]
```

```python
from contextlib import ExitStack

import concourse.bass as bass
from concourse import mybir

F32, F16, I32 = mybir.dt.float32, mybir.dt.float16, mybir.dt.int32
ALU = mybir.AluOpType
ACT = mybir.ActivationFunctionType
AX = mybir.AxisListType

P = 128
D = 512
CT = D // P
ITEMS = 2
PAIRS = P // ITEMS
HEADS = 8
DH = D // HEADS
PH = HEADS // 2
TOPK = 16
EPS = 1e-5
WS = 64.0
LOGIT = float(D) ** -0.5 / (WS * WS)
TAKEN = -3.0e38
RING = 5
UNROLL = 4
FIRST, LAST = 2, PAIRS - 3
STAGES = 4
LOOPS = (LAST - FIRST + 1) // UNROLL


class Turn:

    def __init__(self, i, t):
        self.i, self.t, self.rolled = i, t, not isinstance(i, int)

    def has(self, d):
        return self.rolled or 0 <= self.t + d < PAIRS

    def count(self, per, events):
        const = per * self.t + events
        if not self.rolled:
            return const
        assert const > 0
        return self.i * (per * UNROLL) + const

    def dma(self, d):
        const = 16 * ((self.t + d) // UNROLL + 1)
        if not self.rolled:
            return const
        return self.i * 16 + const

    def slot(self, d, n):
        return (self.t + d) % n


def wait(eng, sem, value):
    if not isinstance(value, int) or value > 0:
        eng.wait_ge(sem, value)


CHUNKS = ([("z", j) for j in range(4)] + [("qk", 0), ("v", 0), ("v", 1), ("o", 0)]
          + [("qk", 1), ("w", 0), ("o", 1)]
          + [("qk", 2), ("w", 1), ("o", 2)]
          + [("qk", 3), ("y", 0), ("y", 1), ("out", 0), ("out", 1), ("o", 3)])
assert len(CHUNKS) % RING == 0


def chunk_exists(T, kind, j):
    return T.has({"z": 1, "w": 1, "y": 1, "qk": 0, "v": 0, "out": -1, "o": 0 if j >= 2 else -1}[kind])


def turns(engine, emit, before_first_attention=None):
    for t in range(-2, FIRST):
        if t == 0 and before_first_attention:
            before_first_attention()
        emit(Turn(0, t))
    with engine.Fori(0, LOOPS) as i:
        for t in range(FIRST, FIRST + UNROLL):
            emit(Turn(i, t))
    for t in range(FIRST + UNROLL * LOOPS, PAIRS + 1):
        emit(Turn(0, t))


def build(nc, x, adj, adj_t, gnn_wt, gnn_b, pos_w, pos_b, qkv_wt, qk_b, v_b, wo_wt, wo_b, out):
    ctx = ExitStack()
    with ctx:
        def sb(name, shape, dt=F32):
            return ctx.enter_context(nc.sbuf_tensor(name, shape, dt))

        def sem(name):
            return ctx.enter_context(nc.semaphore(name))

        stage = [sb(f"stage{i}", [P, 4 * D]) for i in range(STAGES)]
        gw = [sb(f"gw_{n}", [P, 2 * CT, D], F16) for n in ("hi", "lo")]
        qkvw = [sb(f"qkvw_{n}", [P, CT, 3 * D], F16) for n in ("hi", "lo")]
        wow = [sb(f"wow_{n}", [P, CT, D], F16) for n in ("hi", "lo")]
        adj_i = sb("adj_i", [P, P], I32)
        adjt_i = sb("adjt_i", [P, P], I32)
        adj_f = sb("adj_f", [P, P])
        deg = sb("deg", [P, 1])
        mix = sb("mix", [P, 2 * P], F16)
        ident = sb("ident", [P, P])
        eps_c = sb("eps_c", [P, ITEMS])
        half_c = sb("half_c", [P, ITEMS])
        zero_c = sb("zero_c", [P, ITEMS])
        posw = sb("posw", [P, CT, 3])
        w1p = sb("w1p", [P, CT])
        posb = sb("posb", [P, CT])
        qkb = sb("qkb", [P, 2 * CT])
        vb = sb("vb", [P, CT])
        vb_wide = sb("vb_wide", [P, CT, P])
        degb = sb("degb", [P, D])
        outb = sb("outb", [P, D])
        X = [sb(f"X{i}", [P, ITEMS, D]) for i in range(UNROLL)]
        st1 = sb("st1", [P, ITEMS, 6])
        mv1 = sb("mv1", [P, ITEMS, 2])
        ve1, rstd1, nm1, shift1 = (sb(n, [P, ITEMS]) for n in ("ve1", "rstd1", "nm1", "shift1"))
        st2 = sb("st2", [P, ITEMS, 6])
        mv2 = sb("mv2", [P, ITEMS, 2])
        ve2, rstd2, nm2, shift2 = (sb(n, [P, ITEMS]) for n in ("ve2", "rstd2", "nm2", "shift2"))
        xn = sb("xn", [P, ITEMS, D])
        xh, xl = sb("xh", [P, ITEMS, D], F16), sb("xl", [P, ITEMS, D], F16)
        zf = sb("zf", [P, 4, 4 * P])
        of = sb("of", [P, ITEMS, D])
        vf = sb("vf", [P, ITEMS, D])
        zh, zl = (sb(n, [P, 4, 4 * P], F16) for n in ("zh", "zl"))
        y = sb("y", [P, ITEMS, D])
        yt = sb("yt", [P, CT, ITEMS, P])
        t = sb("t", [P, CT, ITEMS, P])
        ph = [sb(f"ph{i}", [P, CT, ITEMS, P], F16) for i in range(2)]
        pl = [sb(f"pl{i}", [P, CT, ITEMS, P], F16) for i in range(2)]
        vh = [sb(f"vh{i}", [P, ITEMS, D], F16) for i in range(2)]
        vl = [sb(f"vl{i}", [P, ITEMS, D], F16) for i in range(2)]
        qh, ql = (sb(n, [P, 2, ITEMS, P], F16) for n in ("qh", "ql"))
        M = sb("M", [P, 4, P])
        m16 = sb("m16", [P, 4, TOPK])
        d16 = sb("d16", [P, 4, TOPK])
        e16 = sb("e16", [P, 4, TOPK])
        s4, ln4, b4 = (sb(n, [P, 4]) for n in ("s4", "ln4", "b4"))
        E = sb("E", [P, 4, P])
        Pm = sb("Pm", [P, 4, P])
        th, tl = (sb(n, [P, 4, P], F16) for n in ("th", "tl"))
        oh = [sb(f"oh{i}", [P, PH, ITEMS, P], F16) for i in range(2)]
        ol = [sb(f"ol{i}", [P, PH, ITEMS, P], F16) for i in range(2)]
        ring = [ctx.enter_context(nc.psum_tensor(f"ring{i}", [P, D], F32)) for i in range(RING)]
        L = [ctx.enter_context(nc.psum_tensor(f"L{i}", [P, ITEMS, P], F32)) for i in range(2)]
        PT = ctx.enter_context(nc.psum_tensor("PT", [P, 4, P], F32))

        w_load = [sem(f"w_load{i}") for i in range(STAGES)]
        c_load = sem("c_load")
        w_hi = sem("w_hi")
        w_lo = sem("w_lo")
        p_set = sem("p_set")
        v_set = sem("v_set")
        bias_mm = sem("bias_mm")
        ready = sem("ready")
        loaded = [sem(f"loaded{i}") for i in range(UNROLL)]
        stored = [sem(f"stored{i}") for i in range(UNROLL)]
        stat1 = sem("stat1")
        scale1 = sem("scale1")
        xn_done = sem("xn_done")
        xl_done = sem("xl_done")
        xdb_done = sem("xdb_done")
        z_mm, z_hi, z_lo = sem("z_mm"), sem("z_hi"), sem("z_lo")
        w_mm, x1_done = sem("w_mm"), sem("x1_done")
        stat2 = sem("stat2")
        scale2 = sem("scale2")
        y_done = sem("y_done")
        xb_done = sem("xb_done")
        y_mm, y_out, tap1 = sem("y_mm"), sem("y_out"), sem("tap1")
        conv = sem("conv")
        p_hi, p_lo = sem("p_hi"), sem("p_lo")
        v_mm, v_hi, v_lo = sem("v_mm"), sem("v_hi"), sem("v_lo")
        qk_mm, qk_hi, qk_lo = sem("qk_mm"), sem("qk_hi"), sem("qk_lo")
        l_mm = sem("l_mm")
        top = sem("top")
        d_done, e16_done, s_done, ln_done, b_done = (sem(n) for n in
                                                     ("d_done", "e16_done", "s_done", "ln_done", "b_done"))
        e_done, p_done = sem("e_done"), sem("p_done")
        t_mm, t_hi, t_lo = sem("t_mm"), sem("t_hi"), sem("t_lo")
        o_mm, o_hi, o_lo = sem("o_mm"), sem("o_hi"), sem("o_lo")
        out_mm, out_f, out_done = sem("out_mm"), sem("out_f"), sem("out_done")

        passed = sem("passed")
        pe_passed = sem("pe_passed")

        def freed(T, kind, j):
            return {"z": lambda: (z_hi, T.count(4, 4 + j + 1)),
                    "qk": lambda: (qk_lo, T.count(4, j + 1)),
                    "o": lambda: (o_lo, T.count(4, j - 2 + 1)),
                    "v": lambda: (v_hi, T.count(2, j + 1)),
                    "w": lambda: (x1_done, T.count(2, 2 + j + 1)),
                    "out": lambda: (out_f, T.count(2, -2 + j + 1)),
                    "y": lambda: (y_out, T.count(2, 2 + j + 1))}[kind]()

        def bank(kind, j):
            return ring[CHUNKS.index((kind, j)) % RING]

        def wait_bank(T, pe, kind, j):
            n = CHUNKS.index((kind, j)) - RING
            while True:
                B = Turn(T.i, T.t + n // len(CHUNKS))
                if B.t < -1 and not B.rolled:
                    return
                before = CHUNKS[n % len(CHUNKS)]
                if chunk_exists(B, *before):
                    wait(pe, *freed(B, *before))
                    return
                n -= RING

        blocks = [(wo_wt[:, :, :], [w[:, :, :] for w in wow]),
                  (gnn_wt[:, 0:CT, :], [w[:, 0:CT, :] for w in gw]),
                  (gnn_wt[:, CT:2 * CT, :], [w[:, CT:2 * CT, :] for w in gw])]
        EARLY = len(blocks)
        blocks += [(qkv_wt[:, :, D * j:D * (j + 1)], [w[:, :, D * j:D * (j + 1)] for w in qkvw]) for j in range(3)]
        NB = len(blocks)

        def staged(n):
            return stage[n % STAGES][:, :].rearrange("p (a b) -> p a b", b=D)

        def arrived(eng, n):
            eng.wait_ge(w_load[n % STAGES], 16 * (n // STAGES + 1))

        smalls = [(adj_i[:, :], adj), (adjt_i[:, :], adj_t), (posw[:, :, :], pos_w), (posb[:, :], pos_b),
                  (qkb[:, :], qk_b), (vb[:, :], v_b), (degb[:, :], gnn_b.to_broadcast((P, D))),
                  (outb[:, :], wo_b.to_broadcast((P, D)))]

        block = ctx.enter_context(nc.Block())

        @block.sync
        def _(sp):
            def load(T, d):
                if not T.has(d):
                    return
                if T.rolled or T.has(d - UNROLL):
                    wait(sp, stored[T.slot(d, UNROLL)], T.dma(d - UNROLL))
                sp.dma_start(X[T.slot(d, UNROLL)][:, :, :], entries(x, T, d)).then_inc(loaded[T.slot(d, UNROLL)], 16)

            def entries(array, T, d):
                a = array.rearrange("(u b) k d -> u k b d", b=ITEMS)
                return a[T.i * UNROLL + (T.t + d)]

            for dst, src in smalls:
                sp.dma_start(dst, src).then_inc(c_load, 16)
            load(Turn(0, -2), 2)
            for n, (src, _) in enumerate(blocks):
                if n >= STAGES:
                    sp.wait_ge(w_lo, n - STAGES + 1)
                if n == EARLY:
                    load(Turn(0, -1), 2)
                sp.dma_start(staged(n), src).then_inc(w_load[n % STAGES], 16)

            def turn(T):
                if T.rolled or T.t >= 0:
                    load(T, 2)
                if T.has(-1):
                    wait(sp, out_done, T.count(2, 0))
                    sp.dma_start(entries(out, T, -1), X[T.slot(-1, UNROLL)][:, :, :])\
                        .then_inc(stored[T.slot(-1, UNROLL)], 16)

            turns(sp, turn)
            for j in range(UNROLL):
                sp.wait_ge(stored[j], 16 * (PAIRS // UNROLL))

        @block.tensor
        def _(pe):
            mm = nc.tensor.matmul

            pe.wait_ge(v_set, 2)
            arrived(pe, 0)
            wo_f = staged(0)
            for c in range(CT):
                last = mm(ring[0][:, :], vb_wide[:, c, :], wo_f[:, c, :], start=c == 0, stop=c == CT - 1)
            last.then_inc(bias_mm, 1)
            pe.wait_ge(ready, 1)

            def three(dst, a, b, first, last):
                mm(dst, a[0], b[0], start=first, stop=False)
                mm(dst, a[0], b[1], start=False, stop=False)
                return mm(dst, a[1], b[0], start=False, stop=last)

            def mix_tokens(T, j):
                item, half = divmod(j, 2)
                if j == 0:
                    wait(pe, xl_done, T.count(1, 2))
                wait_bank(T, pe, "z", j)
                dst = bank("z", j)[:, :].rearrange("p (a b) -> p a b", a=2)
                for a in range(2):
                    c = 2 * half + a
                    mm(dst[:, a, :], xh[:, item, c * P:(c + 1) * P], mix[:, :], start=True, stop=False)
                    last = mm(dst[:, a, :], xl[:, item, c * P:(c + 1) * P], mix[:, :], start=False, stop=True)
                last.then_inc(z_mm, 1)

            def graph_weights(T, item):
                if not T.rolled and T.t == -1 and item == 0:
                    pe.wait_ge(w_lo, EARLY)
                wait(pe, z_lo, T.count(4, 4 + 2 * item + 2))
                wait_bank(T, pe, "w", item)
                for n in range(2 * CT):
                    side, c = divmod(n, CT)
                    col = (c % 2) * 2 * P + side * P
                    lhs = [z[:, 2 * item + c // 2, col:col + P] for z in (zh, zl)]
                    last = three(bank("w", item)[:, :], lhs, [w[:, n, :] for w in gw], n == 0, n == 2 * CT - 1)
                last.then_inc(w_mm, 1)

            def turn_y(T, j):
                wait(pe, y_done, T.count(2, 4))
                wait_bank(T, pe, "y", j)
                dst = bank("y", j)[:, :].rearrange("p (a i k) -> p a i k", a=2, i=ITEMS)
                for a in range(2):
                    for item in range(ITEMS):
                        c = 2 * j + a
                        last = nc.tensor.transpose(dst[:, a, item, :], y[:, item, c * P:(c + 1) * P], ident[:, :])
                last.then_inc(y_mm, 1)

            def values(T, item):
                wait(pe, p_lo, T.count(2, 2))
                wait_bank(T, pe, "v", item)
                s = T.slot(0, 2)
                for c in range(CT):
                    last = three(bank("v", item)[:, :], [a[s][:, c, item, :] for a in (ph, pl)],
                                 [w[:, c, 2 * D:3 * D] for w in qkvw], c == 0, c == CT - 1)
                last.then_inc(v_mm, 1)

            def queries_keys(T, f):
                wait(pe, p_hi, T.count(2, 2))
                wait_bank(T, pe, "qk", f)
                s = T.slot(0, 2)
                for side in range(2):
                    col = side * D + f * P
                    dst = bank("qk", f)[:, side * 2 * P:(side + 1) * 2 * P]
                    for n in range(2 * CT):
                        c, w = divmod(n, 2)
                        mm(dst, qkvw[w][:, c, col:col + P], ph[s][:, c, :, :], start=n == 0, stop=False)
                    if f == 0 and side == 0:
                        wait(pe, p_lo, T.count(2, 2))
                    for c in range(CT):
                        last = mm(dst, qkvw[0][:, c, col:col + P], pl[s][:, c, :, :], start=False, stop=c == CT - 1)
                last.then_inc(qk_mm, 1)

            def logits(T, f):
                wait(pe, e_done, T.count(4, f))
                wait(pe, qk_lo, T.count(4, f + 1))
                if T.rolled:
                    pe.sem_inc(pe_passed, 1)
                for item in range(ITEMS):
                    for h in range(2):
                        r = slice(h * DH, (h + 1) * DH)
                        last = three(L[h][:, item, :], [a[r, 0, item, :] for a in (qh, ql)],
                                     [a[r, 1, item, :] for a in (qh, ql)], True, True)
                last.then_inc(l_mm, 1)

            def turn_probs(T, f):
                wait(pe, p_done, T.count(4, f))
                wait(pe, t_lo, T.count(4, f - 1))
                for j in range(4):
                    last = nc.tensor.transpose(PT[:, j, :], Pm[:, j, :], ident[:, :])
                last.then_inc(t_mm, 1)

            def weighted_values(T, f):
                s = T.slot(0 if f >= 2 else -1, 2)
                head = 2 * ((f - 2) % PH)
                wait(pe, v_lo, T.count(2, 2 if f >= 2 else 0))
                wait(pe, t_lo, T.count(4, f - 1))
                wait_bank(T, pe, "o", f)
                for item in range(ITEMS):
                    for h in range(2):
                        col = slice((head + h) * DH, (head + h + 1) * DH)
                        last = three(bank("o", f)[h * DH:(h + 1) * DH, item * P:(item + 1) * P],
                                     [v[s][:, item, col] for v in (vh, vl)],
                                     [a[:, 2 * item + h, :] for a in (th, tl)], True, True)
                last.then_inc(o_mm, 1)

            def project(T, item):
                s = T.slot(-1, 2)
                wait(pe, o_lo, T.count(4, 0))
                wait_bank(T, pe, "out", item)
                for c in range(CT):
                    last = three(bank("out", item)[:, :], [o[s][:, c, item, :] for o in (oh, ol)],
                                 [w[:, c, :] for w in wow], c == 0, c == CT - 1)
                last.then_inc(out_mm, 1)

            def turn(T):
                for f in range(PH):
                    if f == 0 and T.has(1):
                        for j in range(4):
                            mix_tokens(T, j)
                    if T.has(0):
                        queries_keys(T, f)
                    if f == 0 and T.has(0):
                        values(T, 0)
                        values(T, 1)
                    if f in (1, 2) and T.has(1):
                        graph_weights(T, f - 1)
                    if f == 3 and T.has(1):
                        turn_y(T, 0)
                        turn_y(T, 1)
                    if f == 3 and T.has(-1):
                        project(T, 0)
                        project(T, 1)
                    if T.has(0 if f >= 2 else -1):
                        weighted_values(T, f)
                    if T.has(0):
                        logits(T, f)
                    if T.has(0 if f >= 1 else -1):
                        turn_probs(T, f)

            turns(pe, turn, before_first_attention=lambda: pe.wait_ge(w_lo, NB))

        @block.scalar
        def _(act):
            op = nc.scalar.activation
            nc.scalar.preload_act_table_set("natural_log_exp_and_others")

            def weights_hi(n0, n1):
                for n in range(n0, n1):
                    arrived(act, n)
                    op(blocks[n][1][0], staged(n), ACT.Copy, scale=WS).then_inc(w_hi, 1)

            weights_hi(0, EARLY)
            act.wait_ge(ready, 1)

            def normalize1(T):
                Xu = X[T.slot(2, UNROLL)]
                wait(act, scale1, T.count(4, 12))
                wait(act, xl_done, T.count(1, 2))
                for item in range(ITEMS):
                    op(xn[:, item, :], Xu[:, item, :], ACT.Identity, scale=rstd1[:, item:item + 1],
                       bias=shift1[:, item:item + 1]).then_inc(xn_done, 1)

            def x_split(T):
                wait(act, z_mm, T.count(4, 8))
                wait(act, xn_done, T.count(3, 8))
                op(xh[:, :, :], xn[:, :, :], ACT.Copy).then_inc(xn_done, 1)

            def z_split(T, j):
                wait(act, z_mm, T.count(4, 4 + j + 1))
                if j == 0:
                    wait(act, w_mm, T.count(2, 2))
                    wait(act, z_lo, T.count(4, 4))
                op(zh[:, j, :], bank("z", j)[:, :], ACT.Copy)
                op(zf[:, j, :], bank("z", j)[:, :], ACT.Copy).then_inc(z_hi, 1)

            def normalize2(T, item):
                wait(act, scale2, T.count(8, 8 + 4 * item + 4))
                if item == 0:
                    wait(act, y_mm, T.count(2, 2))
                op(y[:, item, :], X[T.slot(1, UNROLL)][:, item, :], ACT.Identity, scale=rstd2[:, item:item + 1],
                   bias=shift2[:, item:item + 1]).then_inc(y_done, 1)

            def fetch_y(T, j):
                wait(act, y_mm, T.count(2, 2 + j + 1))
                wait(act, conv, T.count(8, 4 * (j + 1)))
                op(yt[:, 2 * j:2 * j + 2, :, :], bank("y", j)[:, :].rearrange("p (a i k) -> p a i k", a=2, i=ITEMS),
                   ACT.Copy).then_inc(y_out, 1)

            def middle_tap(T, j):
                wait(act, y_out, T.count(2, 2 + j + 1))
                wait(act, p_lo, T.count(2, j + 1))
                for a in range(2):
                    c = 2 * j + a
                    last = op(t[:, c, :, :], yt[:, c, :, :], ACT.Identity, scale=w1p[:, c:c + 1],
                              bias=posb[:, c:c + 1])
                last.then_inc(tap1, 1)

            def pos_split(T, j):
                wait(act, conv, T.count(8, 8 + 4 * (j + 1)))
                wait(act, qk_mm, T.count(4, 0))
                op(ph[T.slot(1, 2)][:, 2 * j:2 * j + 2, :, :], t[:, 2 * j:2 * j + 2, :, :], ACT.Copy).then_inc(p_hi, 1)

            def v_split(T, item):
                wait(act, v_mm, T.count(2, item + 1))
                wait(act, o_mm, T.count(4, -4))
                if item == 0:
                    wait(act, v_lo, T.count(2, 0))
                op(vh[T.slot(0, 2)][:, item, :], bank("v", item)[:, :], ACT.Copy)
                op(vf[:, item, :], bank("v", item)[:, :], ACT.Copy).then_inc(v_hi, 1)

            def fetch_out(T, item):
                wait(act, out_mm, T.count(2, -2 + item + 1))
                wait(act, out_done, T.count(2, -4 + item + 1))
                op(of[:, item, :], bank("out", item)[:, :], ACT.Copy, scale=1 / (WS * WS)).then_inc(out_f, 1)

            def qk_split(T, f):
                wait(act, qk_mm, T.count(4, f + 1))
                wait(act, l_mm, T.count(4, f))
                for side in range(2):
                    n = side * CT + f
                    last = op(qh[:, side, :, :], bank("qk", f)[:, side * 2 * P:(side + 1) * 2 * P], ACT.Identity,
                              bias=qkb[:, n:n + 1])
                last.then_inc(qk_hi, 1)

            def soft_sum(T, f):
                wait(act, d_done, T.count(4, f))
                wait(act, s_done, T.count(4, f - 1))
                op(e16[:, :, :], d16[:, :, :], ACT.Exp, scale=LOGIT).then_inc(e16_done, 1)

            def soft_log(T, f):
                wait(act, s_done, T.count(4, f))
                wait(act, b_done, T.count(4, f - 1))
                op(ln4[:, :], s4[:, :], ACT.Ln).then_inc(ln_done, 1)

            def soft_exp(T, f):
                wait(act, b_done, T.count(4, f))
                wait(act, p_done, T.count(4, f - 1))
                for j in range(4):
                    item, h = divmod(j, 2)
                    last = op(E[:, j, :], L[h][:, item, :], ACT.Exp, scale=LOGIT, bias=b4[:, j:j + 1])
                last.then_inc(e_done, 1)

            def probs_split(T, f):
                wait(act, t_mm, T.count(4, f))
                wait(act, o_mm, T.count(4, f - 1))
                op(th[:, :, :], PT[:, :, :], ACT.Copy).then_inc(t_hi, 1)

            def o_split(T, f):
                s = T.slot(0 if f >= 2 else -1, 2)
                wait(act, o_mm, T.count(4, f - 1))
                if f == 2:
                    wait(act, out_mm, T.count(2, -2))
                op(oh[s][:, (f - 2) % PH, :, :], bank("o", f)[:, 0:ITEMS * P], ACT.Copy).then_inc(o_hi, 1)

            def turn(T):
                for f in range(PH):
                    softmax = T.has(0 if f >= 1 else -1)
                    if f == 3 and T.has(1):
                        normalize2(T, 1)
                    if f == 0 and T.has(1):
                        z_split(T, 0)
                        z_split(T, 1)
                    if softmax:
                        soft_sum(T, f)
                    if f == 0 and T.has(1):
                        z_split(T, 2)
                        z_split(T, 3)
                    if T.has(0):
                        qk_split(T, f)
                    if softmax:
                        soft_log(T, f)
                    if f == 3 and T.has(1):
                        fetch_y(T, 0)
                        middle_tap(T, 0)
                    if softmax:
                        soft_exp(T, f)
                    if f == 0 and T.has(0):
                        v_split(T, 0)
                        v_split(T, 1)
                    if f == 2 and T.has(1):
                        normalize2(T, 0)
                    if f == 2 and T.has(2):
                        x_split(T)
                    if f == 3 and T.has(1):
                        fetch_y(T, 1)
                        middle_tap(T, 1)
                    if f == 3 and T.has(-1):
                        fetch_out(T, 0)
                    if f == 3 and T.has(1):
                        pos_split(T, 0)
                    if f == 3 and T.has(-1):
                        fetch_out(T, 1)
                    if T.has(0 if f >= 2 else -1):
                        o_split(T, f)
                    if softmax:
                        probs_split(T, f)
                    if f == 1 and T.has(2):
                        normalize1(T)
                    if f == 3 and T.has(1):
                        pos_split(T, 1)

            turns(act, turn, before_first_attention=lambda: weights_hi(EARLY, NB))

        @block.vector
        def _(dve):
            stt, tt = nc.vector.scalar_tensor_tensor, nc.vector.tensor_tensor

            dve.wait_ge(c_load, 16 * len(smalls))
            dve.wait_ge(p_set, 3)
            nc.vector.memset(vb_wide[:, :, :], 1.0).then_inc(v_set, 1)
            dve.wait_ge(v_set, 1)
            tt(vb_wide[:, :, :], vb_wide[:, :, :], vb[:, :].rearrange("p (c o) -> p c o", o=1).to_broadcast((P, CT, P)),
               ALU.mult).then_inc(v_set, 1)
            nc.vector.tensor_copy(adj_f[:, :], adj_i[:, :]).then_inc(v_set, 1)
            nc.vector.tensor_copy(mix[:, P:2 * P], adjt_i[:, :])
            nc.vector.tensor_scalar(w1p[:, :], posw[:, :, 1], 1.0, None, ALU.add)
            nc.vector.tensor_scalar(qkb[:, :], qkb[:, :], WS, None, ALU.mult)
            dve.wait_ge(v_set, 3)
            nc.vector.tensor_reduce(deg[:, :], adj_f[:, :], AX.X, ALU.add).then_inc(v_set, 1)
            dve.wait_ge(v_set, 4)
            nc.vector.tensor_scalar(mix[:, 0:P], ident[:, :], deg[:, 0:1], None, ALU.mult)
            nc.vector.tensor_scalar(degb[:, :], degb[:, :], deg[:, 0:1], None, ALU.mult)
            dve.wait_ge(bias_mm, 1)
            tt(outb[:, :], ring[0][:, :], outb[:, :], ALU.add).then_inc(ready, 1)

            def weights_lo(n0, n1):
                for n in range(n0, n1):
                    dve.wait_ge(w_hi, n + 1)
                    dst = blocks[n][1]
                    stt(out=dst[1], in0=staged(n), scalar=WS, in1=dst[0], op0=ALU.mult, op1=ALU.subtract)\
                        .then_inc(w_lo, 1)

            weights_lo(0, EARLY)
            dve.wait_ge(w_lo, EARLY)

            def apart(sem, value):
                if not isinstance(value, int) or value > 0:
                    dve.wait_ge(sem, value)
                    dve.sem_inc(passed, 1)

            def stats1(T):
                Xu = X[T.slot(2, UNROLL)]
                wait(dve, scale1, T.count(4, 8))
                apart(loaded[T.slot(2, UNROLL)], T.dma(2))
                for item in range(ITEMS):
                    nc.vector.bn_stats(st1[:, item, :], Xu[:, item, :]).then_inc(stat1, 1)
                for item in range(ITEMS):
                    apart(stat1, T.count(4, 8 + item + 1))
                    nc.vector.bn_aggr(mv1[:, item, :], st1[:, item, :]).then_inc(stat1, 1)

            def residual(T, item):
                Xu = X[T.slot(1, UNROLL)]
                wait(dve, xdb_done, T.count(1, 2))
                wait(dve, w_mm, T.count(2, 2 + item + 1))
                stt(out=Xu[:, item, :], in0=bank("w", item)[:, :], scalar=1 / WS, in1=Xu[:, item, :], op0=ALU.mult,
                    op1=ALU.add).then_inc(x1_done, 1)

            def stats2(T, item):
                Xu = X[T.slot(1, UNROLL)]
                wait(dve, scale2, T.count(8, 4 * item + 4))
                apart(x1_done, T.count(2, 2 + item + 1))
                nc.vector.bn_stats(st2[:, item, :], Xu[:, item, :]).then_inc(stat2, 1)
                apart(stat2, T.count(4, 4 + 2 * item + 1))
                nc.vector.bn_aggr(mv2[:, item, :], st2[:, item, :]).then_inc(stat2, 1)

            def outer_taps(T, j):
                wait(dve, tap1, T.count(2, 2 + j + 1))
                for a in range(2):
                    c = 2 * j + a
                    stt(out=t[:, c, :, 1:P], in0=yt[:, c, :, 0:P - 1], scalar=posw[:, c, 0:1], in1=t[:, c, :, 1:P],
                        op0=ALU.mult, op1=ALU.add).then_inc(conv, 1)
                for a in range(2):
                    c = 2 * j + a
                    wait(dve, conv, T.count(8, 8 + 4 * j + a + 1))
                    stt(out=t[:, c, :, 0:P - 1], in0=yt[:, c, :, 1:P], scalar=posw[:, c, 2:3],
                        in1=t[:, c, :, 0:P - 1], op0=ALU.mult, op1=ALU.add).then_inc(conv, 1)

            def qk_split(T, f):
                wait(dve, qk_hi, T.count(4, f + 1))
                for side in range(2):
                    n = side * CT + f
                    last = stt(out=ql[:, side, :, :], in0=bank("qk", f)[:, side * 2 * P:(side + 1) * 2 * P],
                               scalar=qkb[:, n:n + 1], in1=qh[:, side, :, :], op0=ALU.add, op1=ALU.subtract)
                last.then_inc(qk_lo, 1)

            def select(T, f):
                n = 16 * (f - 1)

                def of(j):
                    item, h = divmod(j, 2)
                    return L[h][:, item, :]

                wait(dve, ln_done, T.count(4, f - 1))
                apart(l_mm, T.count(4, f))
                for j in range(4):
                    nc.vector.max(m16[:, j, 0:8], of(j)).then_inc(top, 1)
                for j in range(4):
                    if j in (0, 3):
                        apart(top, T.count(64, n + (3 if j == 0 else 4)))
                    nc.vector.match_replace(M[:, j, :], m16[:, j, 0:8], of(j), TAKEN).then_inc(top, 1)

            def select_rest(T, f):
                n = 16 * (f - 1)
                for j in range(4):
                    if j in (0, 3):
                        apart(top, T.count(64, n + 4 + (3 if j == 0 else 4)))
                    nc.vector.max(m16[:, j, 8:16], M[:, j, :]).then_inc(top, 1)
                for j in range(4):
                    if j in (0, 3):
                        apart(top, T.count(64, n + 8 + (3 if j == 0 else 4)))
                    nc.vector.match_replace(M[:, j, :], m16[:, j, 8:16], M[:, j, :], TAKEN).then_inc(top, 1)
                wait(dve, e16_done, T.count(4, f - 1))
                tt(d16[:, :, :], m16[:, :, :], m16[:, :, 0:1].to_broadcast((P, 4, TOPK)), ALU.subtract)\
                    .then_inc(d_done, 1)

            def soft_sum(T, f):
                wait(dve, e16_done, T.count(4, f))
                nc.vector.tensor_reduce(s4[:, :], e16[:, :, :], AX.X, ALU.add).then_inc(s_done, 1)

            def soft_bias(T, f):
                wait(dve, ln_done, T.count(4, f))
                wait(dve, e_done, T.count(4, f - 1))
                stt(out=b4[:, :], in0=m16[:, :, 0], scalar=-LOGIT, in1=ln4[:, :], op0=ALU.mult, op1=ALU.subtract)\
                    .then_inc(b_done, 1)

            def keep(T, f):
                wait(dve, e_done, T.count(4, f))
                wait(dve, t_mm, T.count(4, f - 1))
                stt(out=Pm[:, :, :], in0=M[:, :, :], scalar=TAKEN, in1=E[:, :, :], op0=ALU.is_equal, op1=ALU.mult)\
                    .then_inc(p_done, 1)

            def probs_split(T, f):
                wait(dve, t_hi, T.count(4, f))
                tt(tl[:, :, :], PT[:, :, :], th[:, :, :], ALU.subtract).then_inc(t_lo, 1)

            def o_split(T, f):
                s = T.slot(0 if f >= 2 else -1, 2)
                wait(dve, o_hi, T.count(4, f - 1))
                tt(ol[s][:, (f - 2) % PH, :, :], bank("o", f)[:, 0:ITEMS * P].rearrange("p (i k) -> p i k", i=ITEMS),
                   oh[s][:, (f - 2) % PH, :, :], ALU.subtract).then_inc(o_lo, 1)

            def turn(T):
                for f in range(PH):
                    softmax = T.has(0 if f >= 1 else -1)
                    if softmax:
                        soft_sum(T, f)
                    if T.has(0):
                        qk_split(T, f)
                    if softmax:
                        soft_bias(T, f)
                    if f == 1 and T.has(2):
                        stats1(T)
                    if f == 3 and T.has(1):
                        outer_taps(T, 0)
                    if softmax:
                        keep(T, f)
                    if f in (1, 2) and T.has(1):
                        residual(T, f - 1)
                    if f == 2 and T.has(1):
                        stats2(T, 1)
                    if f == 3 and T.has(1):
                        outer_taps(T, 1)
                    if T.has(0 if f >= 2 else -1):
                        o_split(T, f)
                    if T.has(0):
                        select(T, f + 1)
                    if T.has(0):
                        select_rest(T, f + 1)
                    if softmax:
                        probs_split(T, f)
                    if f == 1 and T.has(1):
                        stats2(T, 0)

            turns(dve, turn, before_first_attention=lambda: weights_lo(EARLY, NB))

        @block.gpsimd
        def _(pool):
            tt = nc.gpsimd.tensor_tensor
            nc.gpsimd.memset(ident[:, :], 0.0).then_inc(p_set, 1)
            nc.gpsimd.memset(eps_c[:, :], EPS)
            nc.gpsimd.memset(zero_c[:, :], 0.0)
            nc.gpsimd.memset(half_c[:, :], -0.5).then_inc(p_set, 1)
            pool.wait_ge(p_set, 2)
            nc.gpsimd.affine_select(out=ident[:, :], in_=ident[:, :], compare_op=ALU.not_equal, fill=1.0, base=0,
                                    pattern=[[-1, P]], channel_multiplier=1).then_inc(p_set, 1)
            pool.wait_ge(ready, 1)

            def scales(T, mv, ve, rstd, nm, shift, sem, per, at):
                tt(ve, mv[1], eps_c[:, 0:ve.shape[1]], ALU.add).then_inc(sem, 1)
                wait(pool, sem, T.count(per, at + 1))
                tt(rstd, ve, half_c[:, 0:ve.shape[1]], ALU.pow).then_inc(sem, 1)
                wait(pool, sem, T.count(per, at + 2))
                tt(nm, mv[0], rstd, ALU.mult).then_inc(sem, 1)
                wait(pool, sem, T.count(per, at + 3))
                tt(shift, zero_c[:, 0:ve.shape[1]], nm, ALU.subtract).then_inc(sem, 1)

            def scales1(T):
                wait(pool, stat1, T.count(4, 12))
                wait(pool, xn_done, T.count(3, 6))
                scales(T, (mv1[:, :, 0], mv1[:, :, 1]), ve1[:, :], rstd1[:, :], nm1[:, :], shift1[:, :], scale1, 4, 8)

            def x_split(T):
                wait(pool, xn_done, T.count(3, 9))
                wait(pool, z_mm, T.count(4, 8))
                tt(xl[:, :, :], xn[:, :, :], xh[:, :, :], ALU.subtract).then_inc(xl_done, 1)

            def add_graph_bias(T):
                wait(pool, xn_done, T.count(3, 5))
                Xu = X[T.slot(1, UNROLL)]
                for item in range(ITEMS):
                    last = tt(Xu[:, item, :], Xu[:, item, :], degb[:, :], ALU.add)
                last.then_inc(xdb_done, 1)

            def z_split(T, j):
                wait(pool, w_mm, T.count(2, 2))
                wait(pool, z_hi, T.count(4, 4 + j + 1))
                tt(zl[:, j, :], zf[:, j, :], zh[:, j, :], ALU.subtract).then_inc(z_lo, 1)

            def v_split(T, item):
                s = T.slot(0, 2)
                wait(pool, o_mm, T.count(4, -4))
                wait(pool, v_hi, T.count(2, item + 1))
                tt(vl[s][:, item, :], vf[:, item, :], vh[s][:, item, :], ALU.subtract).then_inc(v_lo, 1)

            def scales2(T, item):
                r = slice(item, item + 1)
                wait(pool, stat2, T.count(4, 4 + 2 * item + 2))
                wait(pool, y_done, T.count(2, item + 1))
                scales(T, (mv2[:, r, 0], mv2[:, r, 1]), ve2[:, r], rstd2[:, r], nm2[:, r], shift2[:, r], scale2, 8,
                       8 + 4 * item)

            def add_out_bias(T, item):
                wait(pool, y_done, T.count(2, 2 + item + 1))
                Xu = X[T.slot(1, UNROLL)]
                tt(Xu[:, item, :], Xu[:, item, :], outb[:, :], ALU.add).then_inc(xb_done, 1)

            def finish(T, item):
                Xu = X[T.slot(-1, UNROLL)]
                wait(pool, out_f, T.count(2, -2 + item + 1))
                tt(Xu[:, item, :], Xu[:, item, :], of[:, item, :], ALU.add).then_inc(out_done, 1)

            def pos_split(T, j):
                c = slice(2 * j, 2 * j + 2)
                s = T.slot(1, 2)
                wait(pool, p_hi, T.count(2, 2 + j + 1))
                tt(pl[s][:, c, :, :], t[:, c, :, :], ph[s][:, c, :, :], ALU.subtract).then_inc(p_lo, 1)

            def turn(T):
                if T.has(1):
                    for j in range(4):
                        z_split(T, j)
                    add_graph_bias(T)
                if T.has(0):
                    for item in range(ITEMS):
                        v_split(T, item)
                if T.has(2):
                    scales1(T)
                if T.has(1):
                    scales2(T, 0)
                    add_out_bias(T, 0)
                if T.has(2):
                    x_split(T)
                if T.has(1):
                    scales2(T, 1)
                    add_out_bias(T, 1)
                if T.has(-1):
                    finish(T, 0)
                if T.has(1):
                    for j in range(2):
                        pos_split(T, j)
                if T.has(-1):
                    finish(T, 1)
            turns(pool, turn)


_OUT = ("out_0_dram", (P, P, D))


def kernel(x, adj, L0_gnn_W, L0_gnn_b, L0_ffn_pos_w, L0_ffn_pos_b, L0_ffn_qkv_w, L0_ffn_qkv_b, L0_ffn_wo_w,
           L0_ffn_wo_b):
    import numpy as np
    import concourse.bacc as bacc
    from concourse.bass_utils import run_bass_kernel_spmd

    def columns(w):
        w = np.asarray(w)
        return w.T.reshape(w.shape[1] // P, P, w.shape[0]).transpose(1, 0, 2)

    def by_channel(v):
        v = np.asarray(v)
        return v.reshape((v.shape[0] // P, P) + v.shape[1:]).swapaxes(0, 1)

    qkv_b = np.asarray(L0_ffn_qkv_b)
    inputs = {
        "x": x, "adj": adj, "adj_t": np.asarray(adj).T, "gnn_wt": columns(L0_gnn_W),
        "gnn_b": np.asarray(L0_gnn_b).reshape(1, D), "pos_w": by_channel(np.asarray(L0_ffn_pos_w).reshape(D, 3)),
        "pos_b": by_channel(L0_ffn_pos_b), "qkv_wt": columns(L0_ffn_qkv_w), "qk_b": by_channel(qkv_b[:2 * D]),
        "v_b": by_channel(qkv_b[2 * D:]), "wo_wt": columns(L0_ffn_wo_w), "wo_b": np.asarray(L0_ffn_wo_b).reshape(1, D),
    }
    nc = bacc.Bacc("TRN2", target_bir_lowering=False, num_devices=1)
    arrays, args = {}, []
    for name, a in inputs.items():
        a = np.ascontiguousarray(a)
        arrays[f"in_{name}_dram"] = a
        args.append(nc.dram_tensor(f"in_{name}_dram", a.shape, mybir.dt.from_np(a.dtype), kind="ExternalInput").ap())
    args.append(nc.dram_tensor(_OUT[0], _OUT[1], F32, kind="ExternalOutput").ap())
    build(nc, *args)
    return run_bass_kernel_spmd(nc, [arrays], core_ids=[0]).results[0][_OUT[0]]
```

```python
from contextlib import ExitStack

import concourse.bass as bass
from concourse import mybir

F32, F16, I32 = mybir.dt.float32, mybir.dt.float16, mybir.dt.int32
ALU = mybir.AluOpType
ACT = mybir.ActivationFunctionType
AX = mybir.AxisListType

P = 128
D = 512
CT = D // P
ITEMS = 2
PAIRS = P // ITEMS
HEADS = 8
DH = D // HEADS
PH = HEADS // 2
TOPK = 16
EPS = 1e-5
WS = 64.0
LOGIT = float(D) ** -0.5 / (WS * WS)
TAKEN = -3.0e38
RING = 5
UNROLL = 4
FIRST, LAST = 2, PAIRS - 3
STAGES = 4
LOOPS = (LAST - FIRST + 1) // UNROLL

class Turn:

    def __init__(self, i, t):
        self.i, self.t, self.rolled = i, t, not isinstance(i, int)
        self.first = not self.rolled and t == -1

    def has(self, d):
        return self.rolled or 0 <= self.t + d < PAIRS

    def count(self, per, events):
        const = per * self.t + events
        if not self.rolled:
            return const
        assert const > 0
        return self.i * (per * UNROLL) + const

    def after(self, per, events):
        return self.rolled or per * self.t + events > 0

    def dma(self, d, transfers):
        const = 16 * transfers * ((self.t + d) // UNROLL + 1)
        if not self.rolled:
            return const
        return self.i * (16 * transfers) + const

    def slot(self, d, n):
        return (self.t + d) % n

CHUNKS = ([("qk", 0), ("w", 0), ("o", 0)]
          + [("w", 1), ("qk", 1)] + [("z", j) for j in range(4)] + [("o", 1)]
          + [("qk", 2), ("y", 0), ("y", 1), ("out", 0), ("out", 1), ("o", 2)]
          + [("qk", 3), ("v", 0), ("v", 1), ("o", 3)])
assert len(CHUNKS) % RING == 0

def chunk_exists(T, kind, j):
    return T.has({"z": 2, "w": 1, "y": 1, "v": 1, "qk": 0, "out": -1, "o": 0 if j >= 2 else -1}[kind])

def turns(engine, emit, before={}):
    for t in range(-2, FIRST):
        if t in before:
            before[t]()
        emit(Turn(0, t))
    with engine.Fori(0, LOOPS) as i:
        for t in range(FIRST, FIRST + UNROLL):
            emit(Turn(i, t))
    for t in range(FIRST + UNROLL * LOOPS, PAIRS + 1):
        emit(Turn(0, t))

def build(nc, x, adj, adj_t, gnn_wt, gnn_b, pos_w, pos_b, qkv_wt, qk_b, v_b, wo_wt, wo_b, out):
    ctx = ExitStack()
    with ctx:
        def sb(name, shape, dt=F32):
            return ctx.enter_context(nc.sbuf_tensor(name, shape, dt))

        def sem(name):
            return ctx.enter_context(nc.semaphore(name))

        stage = [sb(f"stage{i}", [P, 4 * D]) for i in range(STAGES)]
        gw = [sb(f"gw_{n}", [P, 2 * CT, D], F16) for n in ("hi", "lo")]
        qkvw = [sb(f"qkvw_{n}", [P, CT, 3 * D], F16) for n in ("hi", "lo")]
        wow = [sb(f"wow_{n}", [P, CT, D], F16) for n in ("hi", "lo")]
        adj_i = sb("adj_i", [P, P], I32)
        adjt_i = sb("adjt_i", [P, P], I32)
        adj_f = sb("adj_f", [P, P])
        deg = sb("deg", [P, 1])
        mix = sb("mix", [P, 2 * P], F16)
        ident = sb("ident", [P, P])
        eps_c = sb("eps_c", [P, ITEMS])
        half_c = sb("half_c", [P, ITEMS])
        zero_c = sb("zero_c", [P, ITEMS])
        posw = sb("posw", [P, CT, 3])
        w1p = sb("w1p", [P, CT])
        posb = sb("posb", [P, CT])
        qkb = sb("qkb", [P, 2 * CT])
        vb = sb("vb", [P, CT])
        degb = sb("degb", [P, D])
        outb = sb("outb", [P, D])
        X = [sb(f"X{i}", [P, ITEMS, D]) for i in range(UNROLL)]
        st1 = sb("st1", [P, ITEMS, 6])
        mv1 = sb("mv1", [P, ITEMS, 2])
        ve1, rstd1, nm1, shift1 = (sb(n, [P, ITEMS]) for n in ("ve1", "rstd1", "nm1", "shift1"))
        st2 = sb("st2", [P, ITEMS, 6])
        mv2 = sb("mv2", [P, ITEMS, 2])
        ve2, rstd2, nm2, shift2 = (sb(n, [P, ITEMS]) for n in ("ve2", "rstd2", "nm2", "shift2"))
        xn = sb("xn", [P, ITEMS, D])
        xh, xl = sb("xh", [P, ITEMS, D], F16), sb("xl", [P, ITEMS, D], F16)
        zf = sb("zf", [P, 4, 4 * P])
        of = sb("of", [P, ITEMS, D])
        vf = sb("vf", [P, ITEMS, D])
        zh, zl = (sb(n, [P, 4, 4 * P], F16) for n in ("zh", "zl"))
        y = sb("y", [P, ITEMS, D])
        yt = sb("yt", [P, CT, ITEMS, P])
        t = sb("t", [P, CT, ITEMS, P])
        ph = [sb(f"ph{i}", [P, CT, ITEMS, P], F16) for i in range(2)]
        pl = [sb(f"pl{i}", [P, CT, ITEMS, P], F16) for i in range(2)]
        vh = [sb(f"vh{i}", [P, ITEMS, D], F16) for i in range(2)]
        vl = [sb(f"vl{i}", [P, ITEMS, D], F16) for i in range(2)]
        qh, ql = (sb(n, [P, 2, ITEMS, P], F16) for n in ("qh", "ql"))
        M = sb("M", [P, 4, P])
        m16 = sb("m16", [P, 4, TOPK])
        d16 = sb("d16", [P, 4, TOPK])
        e16 = sb("e16", [P, 4, TOPK])
        s4, ln4, b4 = (sb(n, [P, 4]) for n in ("s4", "ln4", "b4"))
        E = sb("E", [P, 4, P])
        Pm = sb("Pm", [P, 4, P])
        th, tl = (sb(n, [P, 4, P], F16) for n in ("th", "tl"))
        oh = [sb(f"oh{i}", [P, PH, ITEMS, P], F16) for i in range(2)]
        ol = [sb(f"ol{i}", [P, PH, ITEMS, P], F16) for i in range(2)]
        ring = [ctx.enter_context(nc.psum_tensor(f"ring{i}", [P, D], F32)) for i in range(RING)]
        L = [ctx.enter_context(nc.psum_tensor(f"L{i}", [P, ITEMS, P], F32)) for i in range(2)]
        PT = ctx.enter_context(nc.psum_tensor("PT", [P, 4, P], F32))

        w_load = [sem(f"w_load{i}") for i in range(STAGES)]
        c_load = sem("c_load")
        w_hi = sem("w_hi")
        w_lo = sem("w_lo")
        p_set = sem("p_set")
        v_set = sem("v_set")
        ready = sem("ready")
        loaded = [sem(f"loaded{i}") for i in range(UNROLL)]
        stored = [sem(f"stored{i}") for i in range(UNROLL)]
        stat1 = sem("stat1")
        scale1 = sem("scale1")
        xn_done = sem("xn_done")
        xl_done = sem("xl_done")
        xdb_done = sem("xdb_done")
        z_mm, z_hi, z_lo = sem("z_mm"), sem("z_hi"), sem("z_lo")
        w_mm, x1_done = sem("w_mm"), sem("x1_done")
        stat2 = sem("stat2")
        scale2 = sem("scale2")
        y_done = sem("y_done")
        xb_done = sem("xb_done")
        y_mm, y_out, tap1 = sem("y_mm"), sem("y_out"), sem("tap1")
        conv = sem("conv")
        p_hi, p_lo = sem("p_hi"), sem("p_lo")
        v_mm, v_hi, v_lo = sem("v_mm"), sem("v_hi"), sem("v_lo")
        qk_mm, qk_hi, qk_lo = sem("qk_mm"), sem("qk_hi"), sem("qk_lo")
        l_mm = sem("l_mm")
        top = sem("top")
        d_done, e16_done, s_done, ln_done, b_done = (sem(n) for n in
                                                     ("d_done", "e16_done", "s_done", "ln_done", "b_done"))
        e_done, p_done = sem("e_done"), sem("p_done")
        t_mm, t_hi, t_lo = sem("t_mm"), sem("t_hi"), sem("t_lo")
        o_mm, o_hi, o_lo = sem("o_mm"), sem("o_hi"), sem("o_lo")
        out_mm, out_f, out_done = sem("out_mm"), sem("out_f"), sem("out_done")

        passed = sem("passed")
        pe_passed = sem("pe_passed")

        def freed(T, kind, j):
            return {"z": lambda: (z_hi, T.count(4, 8 + j + 1)),
                    "qk": lambda: (qk_lo, T.count(4, j + 1)),
                    "o": lambda: (o_lo, T.count(4, j - 2 + 1)),
                    "v": lambda: (v_hi, T.count(2, 2 + j + 1)),
                    "w": lambda: (x1_done, T.count(2, 2 + j + 1)),
                    "out": lambda: (out_f, T.count(2, -2 + j + 1)),
                    "y": lambda: (y_out, T.count(2, 2 + j + 1))}[kind]()

        def bank(kind, j):
            return ring[CHUNKS.index((kind, j)) % RING]

        def wait_bank(T, pe, kind, j):
            n = CHUNKS.index((kind, j)) - RING
            while True:
                B = Turn(T.i, T.t + n // len(CHUNKS))
                if B.t < -2 and not B.rolled:
                    return
                before = CHUNKS[n % len(CHUNKS)]
                if chunk_exists(B, *before):
                    last_read, value = freed(B, *before)
                    if B.rolled or value > 0:
                        pe.wait_ge(last_read, value)
                    return
                n -= RING

        blocks = [(gnn_wt[:, CT * j:CT * (j + 1), :], [w[:, CT * j:CT * (j + 1), :] for w in gw]) for j in range(2)]
        GRAPH = len(blocks)
        blocks += [(qkv_wt[:, :, D * j:D * (j + 1)], [w[:, :, D * j:D * (j + 1)] for w in qkvw]) for j in (2, 0, 1)]
        VALUES = GRAPH + 1
        QKV = len(blocks)
        blocks += [(wo_wt[:, :, :], [w[:, :, :] for w in wow])]
        NB = len(blocks)

        def staged(n):
            return stage[n % STAGES][:, :].rearrange("p (a b) -> p a b", b=D)

        def arrived(eng, n):
            eng.wait_ge(w_load[n % STAGES], 16 * (n // STAGES + 1))

        smalls = [(adj_i[:, :], adj), (adjt_i[:, :], adj_t), (posw[:, :, :], pos_w), (posb[:, :], pos_b),
                  (qkb[:, :], qk_b), (vb[:, :], v_b), (degb[:, :], gnn_b.to_broadcast((P, D))),
                  (outb[:, :], wo_b.to_broadcast((P, D)))]

        block = ctx.enter_context(nc.Block())

        @block.sync
        def _(sp):
            def load(T, d):
                if not T.has(d):
                    return
                if T.rolled or T.has(d - UNROLL):
                    sp.wait_ge(stored[T.slot(d, UNROLL)], T.dma(d - UNROLL, ITEMS))
                sp.dma_start(X[T.slot(d, UNROLL)][:, :, :], entries(x, T, d)).then_inc(loaded[T.slot(d, UNROLL)], 16)

            def entries(array, T, d):
                a = array.rearrange("(u b) k d -> u k b d", b=ITEMS)
                return a[T.i * UNROLL + (T.t + d)]

            load(Turn(0, -2), 2)
            for dst, src in smalls:
                sp.dma_start(dst, src).then_inc(c_load, 16)
            for n, (src, _) in enumerate(blocks):
                if n >= STAGES:
                    sp.wait_ge(w_lo, n - STAGES + 1)
                if n == GRAPH:
                    load(Turn(0, -1), 2)
                sp.dma_start(staged(n), src).then_inc(w_load[n % STAGES], 16)

            def turn(T):
                if T.rolled or T.t >= 0:
                    load(T, 2)
                if T.has(-1):
                    for item in range(ITEMS):
                        sp.wait_ge(out_done, T.count(2, -2 + item + 1))
                        sp.dma_start(entries(out, T, -1)[:, item, :], X[T.slot(-1, UNROLL)][:, item, :])\
                            .then_inc(stored[T.slot(-1, UNROLL)], 16)

            turns(sp, turn)
            for j in range(UNROLL):
                sp.wait_ge(stored[j], 16 * ITEMS * (PAIRS // UNROLL))

        @block.tensor
        def _(pe):
            mm = nc.tensor.matmul

            pe.wait_ge(ready, 1)

            def three(dst, a, b, first, last):
                mm(dst, a[0], b[0], start=first, stop=False)
                mm(dst, a[0], b[1], start=False, stop=False)
                return mm(dst, a[1], b[0], start=False, stop=last)

            def mix_tokens(T, j):
                item, half = divmod(j, 2)
                if j == 0:
                    if T.after(1, 3):
                        pe.wait_ge(xl_done, T.count(1, 3))
                wait_bank(T, pe, "z", j)
                dst = bank("z", j)[:, :].rearrange("p (a b) -> p a b", a=2)
                for a in range(2):
                    c = 2 * half + a
                    mm(dst[:, a, :], xh[:, item, c * P:(c + 1) * P], mix[:, :], start=True, stop=False)
                    last = mm(dst[:, a, :], xl[:, item, c * P:(c + 1) * P], mix[:, :], start=False, stop=True)
                last.then_inc(z_mm, 1)

            def graph_weights(T, item):
                if T.after(4, 4 + 2 * item + 2):
                    pe.wait_ge(z_lo, T.count(4, 4 + 2 * item + 2))
                wait_bank(T, pe, "w", item)
                for n in range(2 * CT):
                    side, c = divmod(n, CT)
                    if T.first and item == 0 and c == 0:
                        pe.wait_ge(w_lo, side + 1)
                    col = (c % 2) * 2 * P + side * P
                    lhs = [z[:, 2 * item + c // 2, col:col + P] for z in (zh, zl)]
                    last = three(bank("w", item)[:, :], lhs, [w[:, n, :] for w in gw], n == 0, n == 2 * CT - 1)
                last.then_inc(w_mm, 1)

            def turn_y(T, j):
                if T.after(2, 4):
                    pe.wait_ge(y_done, T.count(2, 4))
                wait_bank(T, pe, "y", j)
                dst = bank("y", j)[:, :].rearrange("p (a i k) -> p a i k", a=2, i=ITEMS)
                for a in range(2):
                    for item in range(ITEMS):
                        c = 2 * j + a
                        last = nc.tensor.transpose(dst[:, a, item, :], y[:, item, c * P:(c + 1) * P], ident[:, :])
                last.then_inc(y_mm, 1)

            def values(T, item):
                if T.first and item == 0:
                    pe.wait_ge(w_lo, VALUES)
                if T.after(2, 4):
                    pe.wait_ge(p_hi, T.count(2, 4))
                wait_bank(T, pe, "v", item)
                s = T.slot(1, 2)
                for n in range(2 * CT):
                    c, w = divmod(n, 2)
                    mm(bank("v", item)[:, :], ph[s][:, c, item, :], qkvw[w][:, c, 2 * D:3 * D], start=n == 0,
                       stop=False)
                if item == 0:
                    pe.wait_ge(p_lo, T.count(2, 4))
                for c in range(CT):
                    last = mm(bank("v", item)[:, :], pl[s][:, c, item, :], qkvw[0][:, c, 2 * D:3 * D], start=False,
                              stop=c == CT - 1)
                last.then_inc(v_mm, 1)

            def queries_keys(T, f):
                if T.after(2, 2):
                    pe.wait_ge(p_hi, T.count(2, 2))
                wait_bank(T, pe, "qk", f)
                s = T.slot(0, 2)
                for side in range(2):
                    col = side * D + f * P
                    dst = bank("qk", f)[:, side * 2 * P:(side + 1) * 2 * P]
                    for n in range(2 * CT):
                        c, w = divmod(n, 2)
                        mm(dst, qkvw[w][:, c, col:col + P], ph[s][:, c, :, :], start=n == 0, stop=False)
                    if f == 0 and side == 0:
                        if T.after(2, 2):
                            pe.wait_ge(p_lo, T.count(2, 2))
                    for c in range(CT):
                        last = mm(dst, qkvw[0][:, c, col:col + P], pl[s][:, c, :, :], start=False, stop=c == CT - 1)
                last.then_inc(qk_mm, 1)

            def logits(T, f):
                if T.after(4, f):
                    pe.wait_ge(e_done, T.count(4, f))
                if T.after(4, f + 1):
                    pe.wait_ge(qk_lo, T.count(4, f + 1))
                if T.rolled:
                    pe.sem_inc(pe_passed, 1)
                for item in range(ITEMS):
                    for n, (a, b) in enumerate([(qh, qh), (qh, ql), (ql, qh)]):
                        for h in range(2):
                            r = slice(h * DH, (h + 1) * DH)
                            last = mm(L[h][:, item, :], a[r, 0, item, :], b[r, 1, item, :], start=n == 0, stop=n == 2)
                last.then_inc(l_mm, 1)

            def turn_probs(T, f):
                if T.after(4, f):
                    pe.wait_ge(p_done, T.count(4, f))
                if T.after(4, f - 1):
                    pe.wait_ge(t_lo, T.count(4, f - 1))
                for j in range(4):
                    last = nc.tensor.transpose(PT[:, j, :], Pm[:, j, :], ident[:, :])
                last.then_inc(t_mm, 1)

            def weighted_values(T, f):
                s = T.slot(0 if f >= 2 else -1, 2)
                head = 2 * ((f - 2) % PH)
                if T.after(2, 2 if f >= 2 else 0):
                    pe.wait_ge(v_lo, T.count(2, 2 if f >= 2 else 0))
                if T.after(4, f - 1):
                    pe.wait_ge(t_lo, T.count(4, f - 1))
                wait_bank(T, pe, "o", f)
                for item in range(ITEMS):
                    for n, (v, a) in enumerate([(vh, th), (vh, tl), (vl, th)]):
                        for h in range(2):
                            col = slice((head + h) * DH, (head + h + 1) * DH)
                            last = mm(bank("o", f)[h * DH:(h + 1) * DH, item * P:(item + 1) * P], v[s][:, item, col],
                                      a[:, 2 * item + h, :], start=n == 0, stop=n == 2)
                last.then_inc(o_mm, 1)

            def project(T, item):
                s = T.slot(-1, 2)
                wait_bank(T, pe, "out", item)
                for c in range(CT):
                    if item == 0 and c == 0:
                        pe.wait_ge(o_lo, T.count(4, -1))
                    if item == 0 and c == CT - 1:
                        pe.wait_ge(o_lo, T.count(4, 0))
                    last = three(bank("out", item)[:, :], [o[s][:, c, item, :] for o in (oh, ol)],
                                 [w[:, c, :] for w in wow], c == 0, c == CT - 1)
                last.then_inc(out_mm, 1)

            def turn(T):
                for f in range(PH):
                    if f == 1 and T.has(1):
                        graph_weights(T, 1)
                    if T.has(0):
                        queries_keys(T, f)
                    if f == 0 and T.has(1):
                        graph_weights(T, 0)
                    if f == 1 and T.has(2):
                        for j in range(4):
                            mix_tokens(T, j)
                    if f == 2 and T.has(1):
                        turn_y(T, 0)
                        turn_y(T, 1)
                    if f == 2 and T.has(-1):
                        project(T, 0)
                        project(T, 1)
                    if f == 3 and T.has(1):
                        values(T, 0)
                        values(T, 1)
                    if f == 1 and T.has(0):
                        turn_probs(T, f)
                    if T.has(0 if f >= 2 else -1):
                        weighted_values(T, f)
                    if T.has(0):
                        logits(T, f)
                    if f != 1 and T.has(0 if f >= 1 else -1):
                        turn_probs(T, f)

            turns(pe, turn, before={0: lambda: pe.wait_ge(w_lo, QKV),
                                    1: lambda: pe.wait_ge(w_lo, NB)})

        @block.scalar
        def _(act):
            op = nc.scalar.activation
            nc.scalar.preload_act_table_set("natural_log_exp_and_others")

            def weights_hi(n0, n1):
                for n in range(n0, n1):
                    arrived(act, n)
                    op(blocks[n][1][0], staged(n), ACT.Copy, scale=WS).then_inc(w_hi, 1)

            def normalize1(T):
                Xu = X[T.slot(2, UNROLL)]
                if T.after(4, 12):
                    act.wait_ge(scale1, T.count(4, 12))
                if T.after(1, 2):
                    act.wait_ge(xl_done, T.count(1, 2))
                for item in range(ITEMS):
                    op(xn[:, item, :], Xu[:, item, :], ACT.Identity, scale=rstd1[:, item:item + 1],
                       bias=shift1[:, item:item + 1]).then_inc(xn_done, 1)

            def x_split(T):
                if T.after(4, 8):
                    act.wait_ge(z_mm, T.count(4, 8))
                if T.after(3, 8):
                    act.wait_ge(xn_done, T.count(3, 8))
                op(xh[:, :, :], xn[:, :, :], ACT.Copy).then_inc(xn_done, 1)

            def z_split(T, j):
                if T.after(4, 8 + j + 1):
                    act.wait_ge(z_mm, T.count(4, 8 + j + 1))
                if j == 0:
                    if T.after(2, 4):
                        act.wait_ge(w_mm, T.count(2, 4))
                    if T.after(4, 8):
                        act.wait_ge(z_lo, T.count(4, 8))
                op(zh[:, j, :], bank("z", j)[:, :], ACT.Copy)
                op(zf[:, j, :], bank("z", j)[:, :], ACT.Copy).then_inc(z_hi, 1)

            def normalize2(T, item):
                if T.after(8, 8 + 4 * item + 4):
                    act.wait_ge(scale2, T.count(8, 8 + 4 * item + 4))
                if item == 0:
                    if T.after(2, 2):
                        act.wait_ge(y_mm, T.count(2, 2))
                op(y[:, item, :], X[T.slot(1, UNROLL)][:, item, :], ACT.Identity, scale=rstd2[:, item:item + 1],
                   bias=shift2[:, item:item + 1]).then_inc(y_done, 1)

            def fetch_y(T, j):
                if T.after(2, 2 + j + 1):
                    act.wait_ge(y_mm, T.count(2, 2 + j + 1))
                if T.after(8, 4 * (j + 1)):
                    act.wait_ge(conv, T.count(8, 4 * (j + 1)))
                op(yt[:, 2 * j:2 * j + 2, :, :], bank("y", j)[:, :].rearrange("p (a i k) -> p a i k", a=2, i=ITEMS),
                   ACT.Copy).then_inc(y_out, 1)

            def middle_tap(T, j):
                if T.after(2, 2 + j + 1):
                    act.wait_ge(y_out, T.count(2, 2 + j + 1))
                if T.after(2, j + 1):
                    act.wait_ge(p_lo, T.count(2, j + 1))
                for a in range(2):
                    c = 2 * j + a
                    last = op(t[:, c, :, :], yt[:, c, :, :], ACT.Identity, scale=w1p[:, c:c + 1],
                              bias=posb[:, c:c + 1])
                last.then_inc(tap1, 1)

            def pos_split(T, j):
                if T.after(8, 8 + 4 * (j + 1)):
                    act.wait_ge(conv, T.count(8, 8 + 4 * (j + 1)))
                if T.after(4, 0):
                    act.wait_ge(qk_mm, T.count(4, 0))
                op(ph[T.slot(1, 2)][:, 2 * j:2 * j + 2, :, :], t[:, 2 * j:2 * j + 2, :, :], ACT.Copy).then_inc(p_hi, 1)

            def v_split(T, item):
                if T.after(2, 2 + item + 1):
                    act.wait_ge(v_mm, T.count(2, 2 + item + 1))
                if T.after(4, 0):
                    act.wait_ge(o_mm, T.count(4, 0))
                if item == 0:
                    if T.after(2, 2):
                        act.wait_ge(v_lo, T.count(2, 2))
                op(vh[T.slot(1, 2)][:, item, :], bank("v", item)[:, :], ACT.Copy)
                op(vf[:, item, :], bank("v", item)[:, :], ACT.Copy).then_inc(v_hi, 1)

            def fetch_out(T, item):
                if T.after(2, -2 + item + 1):
                    act.wait_ge(out_mm, T.count(2, -2 + item + 1))
                if T.after(2, -4 + item + 1):
                    act.wait_ge(out_done, T.count(2, -4 + item + 1))
                op(of[:, item, :], bank("out", item)[:, :], ACT.Copy, scale=1 / (WS * WS)).then_inc(out_f, 1)

            def qk_split(T, f):
                if T.after(4, f + 1):
                    act.wait_ge(qk_mm, T.count(4, f + 1))
                if T.after(4, f):
                    act.wait_ge(l_mm, T.count(4, f))
                for side in range(2):
                    n = side * CT + f
                    last = op(qh[:, side, :, :], bank("qk", f)[:, side * 2 * P:(side + 1) * 2 * P], ACT.Identity,
                              bias=qkb[:, n:n + 1])
                last.then_inc(qk_hi, 1)

            def soft_sum(T, f):
                if T.after(4, f):
                    act.wait_ge(d_done, T.count(4, f))
                if T.after(4, f - 1):
                    act.wait_ge(s_done, T.count(4, f - 1))
                op(e16[:, :, :], d16[:, :, :], ACT.Exp, scale=LOGIT).then_inc(e16_done, 1)

            def soft_log(T, f):
                if T.after(4, f):
                    act.wait_ge(s_done, T.count(4, f))
                if T.after(4, f - 1):
                    act.wait_ge(b_done, T.count(4, f - 1))
                op(ln4[:, :], s4[:, :], ACT.Ln).then_inc(ln_done, 1)

            def soft_exp(T, f):
                if T.after(4, f):
                    act.wait_ge(b_done, T.count(4, f))
                if T.after(4, f - 1):
                    act.wait_ge(p_done, T.count(4, f - 1))
                for j in range(4):
                    item, h = divmod(j, 2)
                    last = op(E[:, j, :], L[h][:, item, :], ACT.Exp, scale=LOGIT, bias=b4[:, j:j + 1])
                last.then_inc(e_done, 1)

            def probs_split(T, f):
                if T.after(4, f):
                    act.wait_ge(t_mm, T.count(4, f))
                if T.after(4, f - 1):
                    act.wait_ge(o_mm, T.count(4, f - 1))
                op(th[:, :, :], PT[:, :, :], ACT.Copy).then_inc(t_hi, 1)

            def o_split(T, f):
                s = T.slot(0 if f >= 2 else -1, 2)
                if T.after(4, f - 1):
                    act.wait_ge(o_mm, T.count(4, f - 1))
                if f == 2 and T.after(2, -2):
                    act.wait_ge(out_mm, T.count(2, -2))
                c = (f - 2) % PH
                op(oh[s][:, c, :, :], bank("o", f)[:, 0:ITEMS * P], ACT.Identity, bias=vb[:, c:c + 1])\
                    .then_inc(o_hi, 1)

            def turn(T):
                for f in range(PH):
                    softmax = T.has(0 if f >= 1 else -1)
                    if f in (0, 2, 3) and T.has(0):
                        qk_split(T, f)
                    if f == 2 and T.has(1):
                        fetch_y(T, 0)
                    if softmax:
                        soft_sum(T, f)
                    if f == 2 and T.has(1):
                        fetch_y(T, 1)
                    if softmax:
                        soft_log(T, f)
                    if f == 2 and T.has(1):
                        middle_tap(T, 0)
                    if softmax:
                        soft_exp(T, f)
                    if f == 3 and T.first:
                        weights_hi(QKV, NB)
                    if f == 3 and T.has(1):
                        v_split(T, 0)
                        v_split(T, 1)
                    if f == 1 and T.has(1):
                        normalize2(T, 0)
                    if f == 1 and T.has(0):
                        qk_split(T, f)
                    if f == 1 and T.has(1):
                        normalize2(T, 1)
                    if f == 1 and T.has(2):
                        if T.t == -2:
                            weights_hi(0, 1)
                        z_split(T, 0)
                        z_split(T, 1)
                    if f == 2 and T.has(1):
                        middle_tap(T, 1)
                    if f == 2 and T.has(-1):
                        fetch_out(T, 0)
                    if f == 2 and T.has(1):
                        pos_split(T, 0)
                    if T.has(0 if f >= 2 else -1):
                        o_split(T, f)
                    if f == 2 and T.has(-1):
                        fetch_out(T, 1)
                    if softmax:
                        probs_split(T, f)
                    if f == 2 and T.has(1):
                        pos_split(T, 1)
                    if f == 0 and T.has(2):
                        normalize1(T)
                        x_split(T)
                    if f == 1 and T.has(2):
                        if T.t == -2:
                            weights_hi(1, GRAPH)
                        z_split(T, 2)
                        z_split(T, 3)

            def setup():
                weights_hi(GRAPH, QKV)
                act.wait_ge(ready, 1)

            turns(act, turn, before={-1: setup})

        @block.vector
        def _(dve):
            stt, tt = nc.vector.scalar_tensor_tensor, nc.vector.tensor_tensor

            def setup():
                dve.wait_ge(c_load, 16 * len(smalls))
                dve.wait_ge(p_set, 3)
                nc.vector.tensor_copy(adj_f[:, :], adj_i[:, :]).then_inc(v_set, 1)
                nc.vector.tensor_copy(mix[:, P:2 * P], adjt_i[:, :])
                nc.vector.tensor_scalar(w1p[:, :], posw[:, :, 1], 1.0, None, ALU.add)
                nc.vector.tensor_scalar(qkb[:, :], qkb[:, :], WS, None, ALU.mult)
                nc.vector.tensor_scalar(vb[:, :], vb[:, :], WS, None, ALU.mult)
                dve.wait_ge(v_set, 1)
                nc.vector.tensor_reduce(deg[:, :], adj_f[:, :], AX.X, ALU.add).then_inc(v_set, 1)
                dve.wait_ge(v_set, 2)
                nc.vector.tensor_scalar(mix[:, 0:P], ident[:, :], deg[:, 0:1], None, ALU.mult)
                nc.vector.tensor_scalar(degb[:, :], degb[:, :], deg[:, 0:1], None, ALU.mult).then_inc(ready, 1)
                weights_lo(0, GRAPH)

            def weights_lo(n0, n1):
                for n in range(n0, n1):
                    dve.wait_ge(w_hi, n + 1)
                    dst = blocks[n][1]
                    stt(out=dst[1], in0=staged(n), scalar=WS, in1=dst[0], op0=ALU.mult, op1=ALU.subtract)\
                        .then_inc(w_lo, 1)

            def apart(sem, value):
                if not isinstance(value, int) or value > 0:
                    dve.wait_ge(sem, value)
                    dve.sem_inc(passed, 1)

            def stats1(T):
                Xu = X[T.slot(2, UNROLL)]
                if T.after(4, 8):
                    dve.wait_ge(scale1, T.count(4, 8))
                apart(loaded[T.slot(2, UNROLL)], T.dma(2, 1))
                for item in range(ITEMS):
                    nc.vector.bn_stats(st1[:, item, :], Xu[:, item, :]).then_inc(stat1, 1)
                for item in range(ITEMS):
                    apart(stat1, T.count(4, 8 + item + 1))
                    nc.vector.bn_aggr(mv1[:, item, :], st1[:, item, :]).then_inc(stat1, 1)

            def residual(T, item):
                Xu = X[T.slot(1, UNROLL)]
                if T.after(1, 2):
                    dve.wait_ge(xdb_done, T.count(1, 2))
                if T.after(2, 2 + item + 1):
                    dve.wait_ge(w_mm, T.count(2, 2 + item + 1))
                stt(out=Xu[:, item, :], in0=bank("w", item)[:, :], scalar=1 / WS, in1=Xu[:, item, :], op0=ALU.mult,
                    op1=ALU.add).then_inc(x1_done, 1)

            def stats2(T, item):
                Xu = X[T.slot(1, UNROLL)]
                if T.after(8, 4 * item + 4):
                    dve.wait_ge(scale2, T.count(8, 4 * item + 4))
                apart(x1_done, T.count(2, 2 + item + 1))
                nc.vector.bn_stats(st2[:, item, :], Xu[:, item, :]).then_inc(stat2, 1)
                apart(stat2, T.count(4, 4 + 2 * item + 1))
                nc.vector.bn_aggr(mv2[:, item, :], st2[:, item, :]).then_inc(stat2, 1)

            def outer_taps(T, j):
                if T.after(2, 2 + j + 1):
                    dve.wait_ge(tap1, T.count(2, 2 + j + 1))
                for a in range(2):
                    c = 2 * j + a
                    stt(out=t[:, c, :, 1:P], in0=yt[:, c, :, 0:P - 1], scalar=posw[:, c, 0:1], in1=t[:, c, :, 1:P],
                        op0=ALU.mult, op1=ALU.add).then_inc(conv, 1)
                for a in range(2):
                    c = 2 * j + a
                    if T.after(8, 8 + 4 * j + a + 1):
                        dve.wait_ge(conv, T.count(8, 8 + 4 * j + a + 1))
                    stt(out=t[:, c, :, 0:P - 1], in0=yt[:, c, :, 1:P], scalar=posw[:, c, 2:3],
                        in1=t[:, c, :, 0:P - 1], op0=ALU.mult, op1=ALU.add).then_inc(conv, 1)

            def qk_split(T, f):
                if T.after(4, f + 1):
                    dve.wait_ge(qk_hi, T.count(4, f + 1))
                for side in range(2):
                    n = side * CT + f
                    last = stt(out=ql[:, side, :, :], in0=bank("qk", f)[:, side * 2 * P:(side + 1) * 2 * P],
                               scalar=qkb[:, n:n + 1], in1=qh[:, side, :, :], op0=ALU.add, op1=ALU.subtract)
                last.then_inc(qk_lo, 1)

            def select(T, f):
                n = 16 * (f - 1)

                def of(j):
                    item, h = divmod(j, 2)
                    return L[h][:, item, :]

                if T.after(4, f - 1):
                    dve.wait_ge(ln_done, T.count(4, f - 1))
                apart(l_mm, T.count(4, f))
                for j in range(4):
                    nc.vector.max(m16[:, j, 0:8], of(j)).then_inc(top, 1)
                for j in range(4):
                    if j in (0, 3):
                        apart(top, T.count(64, n + (3 if j == 0 else 4)))
                    nc.vector.match_replace(M[:, j, :], m16[:, j, 0:8], of(j), TAKEN).then_inc(top, 1)

            def select_rest(T, f):
                n = 16 * (f - 1)
                for j in range(4):
                    if j in (0, 3):
                        apart(top, T.count(64, n + 4 + (3 if j == 0 else 4)))
                    nc.vector.max(m16[:, j, 8:16], M[:, j, :]).then_inc(top, 1)
                for j in range(4):
                    if j in (0, 3):
                        apart(top, T.count(64, n + 8 + (3 if j == 0 else 4)))
                    nc.vector.match_replace(M[:, j, :], m16[:, j, 8:16], M[:, j, :], TAKEN).then_inc(top, 1)
                if T.after(4, f - 1):
                    dve.wait_ge(e16_done, T.count(4, f - 1))
                tt(d16[:, :, :], m16[:, :, :], m16[:, :, 0:1].to_broadcast((P, 4, TOPK)), ALU.subtract)\
                    .then_inc(d_done, 1)

            def soft_sum(T, f):
                if T.after(4, f):
                    dve.wait_ge(e16_done, T.count(4, f))
                nc.vector.tensor_reduce(s4[:, :], e16[:, :, :], AX.X, ALU.add).then_inc(s_done, 1)

            def soft_bias(T, f):
                if T.after(4, f):
                    dve.wait_ge(ln_done, T.count(4, f))
                if T.after(4, f - 1):
                    dve.wait_ge(e_done, T.count(4, f - 1))
                stt(out=b4[:, :], in0=m16[:, :, 0], scalar=-LOGIT, in1=ln4[:, :], op0=ALU.mult, op1=ALU.subtract)\
                    .then_inc(b_done, 1)

            def keep(T, f):
                if T.after(4, f):
                    dve.wait_ge(e_done, T.count(4, f))
                if T.after(4, f - 1):
                    dve.wait_ge(t_mm, T.count(4, f - 1))
                stt(out=Pm[:, :, :], in0=M[:, :, :], scalar=TAKEN, in1=E[:, :, :], op0=ALU.is_equal, op1=ALU.mult)\
                    .then_inc(p_done, 1)

            def probs_split(T, f):
                if T.after(4, f):
                    dve.wait_ge(t_hi, T.count(4, f))
                tt(tl[:, :, :], PT[:, :, :], th[:, :, :], ALU.subtract).then_inc(t_lo, 1)

            def o_split(T, f):
                s = T.slot(0 if f >= 2 else -1, 2)
                if T.after(4, f - 1):
                    dve.wait_ge(o_hi, T.count(4, f - 1))
                c = (f - 2) % PH
                stt(out=ol[s][:, c, :, :], in0=bank("o", f)[:, 0:ITEMS * P].rearrange("p (i k) -> p i k", i=ITEMS),
                    scalar=vb[:, c:c + 1], in1=oh[s][:, c, :, :], op0=ALU.add, op1=ALU.subtract).then_inc(o_lo, 1)

            def turn(T):
                for f in range(PH):
                    softmax = T.has(0 if f >= 1 else -1)
                    if softmax:
                        soft_sum(T, f)
                    if f in (0, 2, 3) and T.has(0):
                        qk_split(T, f)
                    if softmax:
                        soft_bias(T, f)
                    if f == 0 and T.has(2):
                        stats1(T)
                    if f == 0 and T.first:
                        weights_lo(GRAPH, QKV)
                    if f == 1 and T.has(1):
                        residual(T, 1)
                        stats2(T, 1)
                    if f == 2 and T.has(1):
                        outer_taps(T, 0)
                    if softmax:
                        keep(T, f)
                    if f == 0 and T.has(1):
                        residual(T, 0)
                    if f == 1 and T.has(0):
                        qk_split(T, f)
                    if f == 2 and T.has(1):
                        outer_taps(T, 1)
                    if T.has(0 if f >= 2 else -1):
                        o_split(T, f)
                    if T.has(0):
                        select(T, f + 1)
                    if T.has(0):
                        select_rest(T, f + 1)
                    if softmax:
                        probs_split(T, f)
                    if f == 0 and T.has(1):
                        stats2(T, 0)

            turns(dve, turn, before={-1: setup, 0: lambda: weights_lo(QKV, NB)})

        @block.gpsimd
        def _(pool):
            tt = nc.gpsimd.tensor_tensor
            nc.gpsimd.memset(ident[:, :], 0.0).then_inc(p_set, 1)
            nc.gpsimd.memset(eps_c[:, :], EPS)
            nc.gpsimd.memset(zero_c[:, :], 0.0)
            nc.gpsimd.memset(half_c[:, :], -0.5).then_inc(p_set, 1)
            pool.wait_ge(p_set, 2)
            nc.gpsimd.affine_select(out=ident[:, :], in_=ident[:, :], compare_op=ALU.not_equal, fill=1.0, base=0,
                                    pattern=[[-1, P]], channel_multiplier=1).then_inc(p_set, 1)

            def scales(T, mv, ve, rstd, nm, shift, sem, per, at):
                tt(ve, mv[1], eps_c[:, 0:ve.shape[1]], ALU.add).then_inc(sem, 1)
                if T.after(per, at + 1):
                    pool.wait_ge(sem, T.count(per, at + 1))
                tt(rstd, ve, half_c[:, 0:ve.shape[1]], ALU.pow).then_inc(sem, 1)
                if T.after(per, at + 2):
                    pool.wait_ge(sem, T.count(per, at + 2))
                tt(nm, mv[0], rstd, ALU.mult).then_inc(sem, 1)
                if T.after(per, at + 3):
                    pool.wait_ge(sem, T.count(per, at + 3))
                tt(shift, zero_c[:, 0:ve.shape[1]], nm, ALU.subtract).then_inc(sem, 1)

            def scales1(T):
                if T.after(4, 12):
                    pool.wait_ge(stat1, T.count(4, 12))
                if T.after(3, 6):
                    pool.wait_ge(xn_done, T.count(3, 6))
                scales(T, (mv1[:, :, 0], mv1[:, :, 1]), ve1[:, :], rstd1[:, :], nm1[:, :], shift1[:, :], scale1, 4, 8)

            def x_split(T):
                if T.after(3, 9):
                    pool.wait_ge(xn_done, T.count(3, 9))
                if T.after(4, 8):
                    pool.wait_ge(z_mm, T.count(4, 8))
                tt(xl[:, :, :], xn[:, :, :], xh[:, :, :], ALU.subtract).then_inc(xl_done, 1)

            def add_graph_bias(T):
                if not T.rolled and T.t == -2:
                    pool.wait_ge(ready, 1)
                if T.after(3, 8):
                    pool.wait_ge(xn_done, T.count(3, 8))
                Xu = X[T.slot(2, UNROLL)]
                for item in range(ITEMS):
                    last = tt(Xu[:, item, :], Xu[:, item, :], degb[:, :], ALU.add)
                last.then_inc(xdb_done, 1)

            def z_split(T, j):
                if T.after(2, 4):
                    pool.wait_ge(w_mm, T.count(2, 4))
                if T.after(4, 8 + j + 1):
                    pool.wait_ge(z_hi, T.count(4, 8 + j + 1))
                tt(zl[:, j, :], zf[:, j, :], zh[:, j, :], ALU.subtract).then_inc(z_lo, 1)

            def v_split(T, item):
                s = T.slot(1, 2)
                if T.after(4, 0):
                    pool.wait_ge(o_mm, T.count(4, 0))
                if T.after(2, 2 + item + 1):
                    pool.wait_ge(v_hi, T.count(2, 2 + item + 1))
                tt(vl[s][:, item, :], vf[:, item, :], vh[s][:, item, :], ALU.subtract).then_inc(v_lo, 1)

            def scales2(T, item):
                r = slice(item, item + 1)
                if T.after(4, 4 + 2 * item + 2):
                    pool.wait_ge(stat2, T.count(4, 4 + 2 * item + 2))
                if T.after(2, item + 1):
                    pool.wait_ge(y_done, T.count(2, item + 1))
                scales(T, (mv2[:, r, 0], mv2[:, r, 1]), ve2[:, r], rstd2[:, r], nm2[:, r], shift2[:, r], scale2, 8,
                       8 + 4 * item)

            def add_out_bias(T, item):
                if T.after(2, 2 + item + 1):
                    pool.wait_ge(y_done, T.count(2, 2 + item + 1))
                Xu = X[T.slot(1, UNROLL)]
                tt(Xu[:, item, :], Xu[:, item, :], outb[:, :], ALU.add).then_inc(xb_done, 1)

            def finish(T, item):
                Xu = X[T.slot(-1, UNROLL)]
                if T.after(2, -2 + item + 1):
                    pool.wait_ge(out_f, T.count(2, -2 + item + 1))
                tt(Xu[:, item, :], Xu[:, item, :], of[:, item, :], ALU.add).then_inc(out_done, 1)

            def pos_split(T, j):
                c = slice(2 * j, 2 * j + 2)
                s = T.slot(1, 2)
                if T.after(2, 2 + j + 1):
                    pool.wait_ge(p_hi, T.count(2, 2 + j + 1))
                tt(pl[s][:, c, :, :], t[:, c, :, :], ph[s][:, c, :, :], ALU.subtract).then_inc(p_lo, 1)

            def turn(T):
                if T.has(2):
                    scales1(T)
                    x_split(T)
                if T.has(1):
                    for item in range(ITEMS):
                        scales2(T, item)
                if T.has(2):
                    for j in range(4):
                        z_split(T, j)
                    add_graph_bias(T)
                if T.has(1):
                    for j in range(2):
                        pos_split(T, j)
                if T.has(-1):
                    for item in range(ITEMS):
                        finish(T, item)
                if T.has(1):
                    for item in range(ITEMS):
                        v_split(T, item)
                    for item in range(ITEMS):
                        add_out_bias(T, item)

            turns(pool, turn)

_OUT = ("out_0_dram", (P, P, D))

def kernel(x, adj, L0_gnn_W, L0_gnn_b, L0_ffn_pos_w, L0_ffn_pos_b, L0_ffn_qkv_w, L0_ffn_qkv_b, L0_ffn_wo_w,
           L0_ffn_wo_b):
    import numpy as np
    import concourse.bacc as bacc
    from concourse.bass_utils import run_bass_kernel_spmd

    def columns(w):
        w = np.asarray(w)
        return w.T.reshape(w.shape[1] // P, P, w.shape[0]).transpose(1, 0, 2)

    def by_channel(v):
        v = np.asarray(v)
        return v.reshape((v.shape[0] // P, P) + v.shape[1:]).swapaxes(0, 1)

    qkv_b = np.asarray(L0_ffn_qkv_b)
    inputs = {
        "x": x, "adj": adj, "adj_t": np.asarray(adj).T, "gnn_wt": columns(L0_gnn_W),
        "gnn_b": np.asarray(L0_gnn_b).reshape(1, D), "pos_w": by_channel(np.asarray(L0_ffn_pos_w).reshape(D, 3)),
        "pos_b": by_channel(L0_ffn_pos_b), "qkv_wt": columns(L0_ffn_qkv_w), "qk_b": by_channel(qkv_b[:2 * D]),
        "v_b": by_channel(qkv_b[2 * D:]), "wo_wt": columns(L0_ffn_wo_w), "wo_b": np.asarray(L0_ffn_wo_b).reshape(1, D),
    }
    nc = bacc.Bacc("TRN2", target_bir_lowering=False, num_devices=1)
    arrays, args = {}, []
    for name, a in inputs.items():
        a = np.ascontiguousarray(a)
        arrays[f"in_{name}_dram"] = a
        args.append(nc.dram_tensor(f"in_{name}_dram", a.shape, mybir.dt.from_np(a.dtype), kind="ExternalInput").ap())
    args.append(nc.dram_tensor(_OUT[0], _OUT[1], F32, kind="ExternalOutput").ap())
    build(nc, *args)
    return run_bass_kernel_spmd(nc, [arrays], core_ids=[0]).results[0][_OUT[0]]
```
